# Optimizing a Trainium2 kernel written in Bass

```python
import numpy as np
import jax
import jax.numpy as jnp

def _softmax(x, axis=-1):
    return jax.nn.softmax(x, axis=axis)

def _gelu(x):
    return jax.nn.gelu(x, approximate=True)

def _silu(x):
    return jax.nn.silu(x)

def _sigmoid(x):
    return jax.nn.sigmoid(x)

def _layernorm(x, axis=-1, eps=1e-05):
    m = jnp.mean(x, axis=axis, keepdims=True)
    v = jnp.var(x, axis=axis, keepdims=True)
    return (x - m) / jnp.sqrt(v + eps)

def _scatter_add(tgt, idx, src, axis=0):
    return tgt.at[idx].add(src)

def _segment_sum(src, seg, n):
    return jax.ops.segment_sum(src, seg, n)
kernel_name = 'mk_vit_tower_d1_tok_img768_r4_3dd9f5'

def setup_inputs(seed: int=0):
    np.random.seed(seed)
    _w = jnp.asarray

    def _rec_inputs():
        import jax
        import jax.numpy as jnp
        _rk = jax.random.key(seed)
        x = -0.00040386 + 0.999972 * jax.random.normal(jax.random.fold_in(_rk, 1), (64, 64, 64, 3), jnp.float32)
        return x
    x = _rec_inputs()

    def _L0_tok_setup():
        import jax, jax.numpy as jnp
        import numpy as np
        PATCH = 16
        key = jax.random.key(seed)
        k1, k2, k3 = jax.random.split(key, 3)
        B, H, Wd, C = (64, 64, 64, 3)
        patch_dim = PATCH * PATCH * C
        hidden = 192
        num_patches = H // PATCH * (Wd // PATCH)
        img = jax.random.normal(k1, (B, H, Wd, C), dtype=jnp.float32)
        W = jax.random.normal(k2, (patch_dim, hidden), dtype=jnp.float32) * (1.0 / np.sqrt(patch_dim))
        b = jnp.zeros((hidden,), dtype=jnp.float32)
        pos_emb = jax.random.normal(k3, (num_patches, hidden), dtype=jnp.float32) * 0.02
        return {'img': img, 'W': W, 'b': b, 'pos_emb': pos_emb}
    _L0_tok_all = _L0_tok_setup()
    _L0_tok_in = {k: v for k, v in _L0_tok_all.items() if k in ('W', 'b', 'pos_emb')}
    del _L0_tok_all

    def _L0_attn_setup():
        import jax, jax.numpy as jnp
        import numpy as np
        FEATS = 192
        HEAD = 12
        HD = FEATS // HEAD
        B, N = (128, 197)
        key = jax.random.key(seed)
        k0, k1, k2 = jax.random.split(key, 3)
        x = jax.random.normal(k0, (B, N, FEATS), dtype=jnp.float32)
        W_qkv = jax.random.normal(k1, (HEAD, HD, 3 * HD), dtype=jnp.float32) * 0.05
        b_qkv = jnp.zeros((HEAD, 3 * HD), dtype=jnp.float32)
        W_out = jax.random.normal(k2, (FEATS, FEATS), dtype=jnp.float32) * 0.02
        b_out = jnp.zeros((FEATS,), dtype=jnp.float32)
        return {'x': x, 'W_qkv': W_qkv, 'b_qkv': b_qkv, 'W_out': W_out, 'b_out': b_out}
    _L0_attn_all = _L0_attn_setup()
    _L0_attn_in = {k: v for k, v in _L0_attn_all.items() if k in ('W_qkv', 'b_qkv', 'W_out', 'b_out')}
    del _L0_attn_all

    def _L0_ffn_setup():
        import jax, jax.numpy as jnp
        import numpy as np
        B, N, D, H, E, HID, TOPK = (8, 197, 192, 12, 8, 768, 2)

        def _layernorm(x, w, b, eps=1e-05):
            mu = jnp.mean(x, axis=-1, keepdims=True)
            var = jnp.mean((x - mu) ** 2, axis=-1, keepdims=True)
            return (x - mu) * jax.lax.rsqrt(var + eps) * w + b
        key = jax.random.key(seed)
        ks = jax.random.split(key, 8)
        s = 0.02
        return {'x': jax.random.normal(ks[0], (B, N, D), jnp.float32), 'norm1_w': jnp.ones((D,), jnp.float32), 'norm1_b': jnp.zeros((D,), jnp.float32), 'qkv_w': jax.random.normal(ks[1], (3 * D, D), jnp.float32) * s, 'qkv_b': jnp.zeros((3 * D,), jnp.float32), 'proj_w': jax.random.normal(ks[2], (D, D), jnp.float32) * s, 'proj_b': jnp.zeros((D,), jnp.float32), 'norm2_w': jnp.ones((D,), jnp.float32), 'norm2_b': jnp.zeros((D,), jnp.float32), 'w_gate': jax.random.normal(ks[3], (D, E), jnp.float32) * s, 'W1': jax.random.normal(ks[4], (E, D, HID), jnp.float32) * s, 'b1': jnp.zeros((E, HID), jnp.float32), 'W2': jax.random.normal(ks[5], (E, HID, D), jnp.float32) * s, 'b2': jnp.zeros((E, D), jnp.float32)}
    _L0_ffn_all = _L0_ffn_setup()
    _L0_ffn_in = {k: v for k, v in _L0_ffn_all.items() if k in ('norm1_w', 'norm1_b', 'qkv_w', 'qkv_b', 'proj_w', 'proj_b', 'norm2_w', 'norm2_b', 'w_gate', 'W1', 'b1', 'W2', 'b2')}
    del _L0_ffn_all
    return {'x': x, 'L0_tok_W': _L0_tok_in['W'], 'L0_tok_b': _L0_tok_in['b'], 'L0_tok_pos_emb': _L0_tok_in['pos_emb'], 'L0_attn_W_qkv': _L0_attn_in['W_qkv'], 'L0_attn_b_qkv': _L0_attn_in['b_qkv'], 'L0_attn_W_out': _L0_attn_in['W_out'], 'L0_attn_b_out': _L0_attn_in['b_out'], 'L0_ffn_norm1_w': _L0_ffn_in['norm1_w'], 'L0_ffn_norm1_b': _L0_ffn_in['norm1_b'], 'L0_ffn_qkv_w': _L0_ffn_in['qkv_w'], 'L0_ffn_qkv_b': _L0_ffn_in['qkv_b'], 'L0_ffn_proj_w': _L0_ffn_in['proj_w'], 'L0_ffn_proj_b': _L0_ffn_in['proj_b'], 'L0_ffn_norm2_w': _L0_ffn_in['norm2_w'], 'L0_ffn_norm2_b': _L0_ffn_in['norm2_b'], 'L0_ffn_w_gate': _L0_ffn_in['w_gate'], 'L0_ffn_W1': _L0_ffn_in['W1'], 'L0_ffn_b1': _L0_ffn_in['b1'], 'L0_ffn_W2': _L0_ffn_in['W2'], 'L0_ffn_b2': _L0_ffn_in['b2']}

def reference(x, L0_tok_W, L0_tok_b, L0_tok_pos_emb, L0_attn_W_qkv, L0_attn_b_qkv, L0_attn_W_out, L0_attn_b_out, L0_ffn_norm1_w, L0_ffn_norm1_b, L0_ffn_qkv_w, L0_ffn_qkv_b, L0_ffn_proj_w, L0_ffn_proj_b, L0_ffn_norm2_w, L0_ffn_norm2_b, L0_ffn_w_gate, L0_ffn_W1, L0_ffn_b1, L0_ffn_W2, L0_ffn_b2):
    import jax
    import jax.numpy as jnp

    def _L0_tok_ref(img, W, b, pos_emb):
        import jax, jax.numpy as jnp
        import numpy as np
        PATCH = 16
        B, H, Wd, C = img.shape
        ph, pw = (H // PATCH, Wd // PATCH)
        p = img.reshape(B, ph, PATCH, pw, PATCH, C)
        p = p.transpose(0, 1, 3, 2, 4, 5).reshape(B, ph * pw, PATCH * PATCH * C)
        out = jnp.einsum('bnk,kh->bnh', p, W) + b + pos_emb[None, :, :]
        return out

    def _L0_attn_ref(x, W_qkv, b_qkv, W_out, b_out):
        import jax, jax.numpy as jnp
        import numpy as np
        FEATS = 192
        HEAD = 12
        HD = FEATS // HEAD
        B, N = (128, 197)
        b, n, f = x.shape
        h, hd = (W_qkv.shape[0], W_qkv.shape[1])
        xh = x.reshape(b, n, h, hd)
        qkv = jnp.einsum('bnhd,hde->bnhe', xh, W_qkv) + b_qkv
        q, k, v = jnp.split(qkv, 3, axis=-1)
        scale = jnp.asarray(f, x.dtype) ** 0.5
        scores = jnp.einsum('bihd,bjhd->bhij', q, k) / scale
        p = jax.nn.softmax(scores, axis=-1)
        attn = jnp.einsum('bhij,bjhd->bihd', p, v)
        out = attn.reshape(b, n, f) @ W_out + b_out
        return out

    def _L0_ffn_ref(x, norm1_w, norm1_b, qkv_w, qkv_b, proj_w, proj_b, norm2_w, norm2_b, w_gate, W1, b1, W2, b2):
        import jax, jax.numpy as jnp
        import numpy as np
        B, N, D, H, E, HID, TOPK = (8, 197, 192, 12, 8, 768, 2)

        def _layernorm(x, w, b, eps=1e-05):
            mu = jnp.mean(x, axis=-1, keepdims=True)
            var = jnp.mean((x - mu) ** 2, axis=-1, keepdims=True)
            return (x - mu) * jax.lax.rsqrt(var + eps) * w + b
        Bx, Nx, C = x.shape
        hd = C // H
        scale = hd ** (-0.5)
        xn = _layernorm(x, norm1_w, norm1_b)
        qkv = (xn @ qkv_w.T + qkv_b).reshape(Bx, Nx, 3, H, hd).transpose(2, 0, 3, 1, 4)
        q, k, v = (qkv[0], qkv[1], qkv[2])
        attn = jax.nn.softmax(jnp.einsum('bhqd,bhkd->bhqk', q, k) * scale, axis=-1)
        o = jnp.einsum('bhqk,bhkd->bqhd', attn, v).reshape(Bx, Nx, C)
        x = x + (o @ proj_w.T + proj_b)
        xn2 = _layernorm(x, norm2_w, norm2_b).reshape(-1, C)
        T = xn2.shape[0]
        logits = xn2 @ w_gate
        top_vals, top_idx = jax.lax.top_k(logits, TOPK)
        gates = jax.nn.softmax(top_vals, axis=-1)
        gates_full = jnp.zeros((T, E), xn2.dtype).at[jnp.arange(T)[:, None], top_idx].add(gates)

        def body(acc, p):
            w1, bb1, w2, bb2, g = p
            h = jax.nn.gelu(xn2 @ w1 + bb1, approximate=False)
            return (acc + g[:, None] * (h @ w2 + bb2), None)
        moe_out, _ = jax.lax.scan(body, jnp.zeros_like(xn2), (W1, b1, W2, b2, gates_full.T))
        return x + moe_out.reshape(Bx, Nx, C)
    h = _L0_tok_ref(x, L0_tok_W, L0_tok_b, L0_tok_pos_emb)
    h = h + _L0_attn_ref(_layernorm(h, axis=-1), L0_attn_W_qkv, L0_attn_b_qkv, L0_attn_W_out, L0_attn_b_out)
    h = h + _L0_ffn_ref(_layernorm(h, axis=-1), L0_ffn_norm1_w, L0_ffn_norm1_b, L0_ffn_qkv_w, L0_ffn_qkv_b, L0_ffn_proj_w, L0_ffn_proj_b, L0_ffn_norm2_w, L0_ffn_norm2_b, L0_ffn_w_gate, L0_ffn_W1, L0_ffn_b1, L0_ffn_W2, L0_ffn_b2)
    return h

_drawn_inputs = setup_inputs


def setup_inputs(seed=0):
    import zlib

    import numpy as np

    out = dict(_drawn_inputs(seed))
    spreads = {'L0_tok_b': (0.0, 0.1),
     'L0_attn_b_qkv': (0.0, 0.283),
     'L0_attn_b_out': (0.0, 0.1),
     'L0_ffn_norm1_w': (1.0, 0.6),
     'L0_ffn_norm1_b': (0.0, 0.8),
     'L0_ffn_qkv_b': (0.0, 0.519),
     'L0_ffn_proj_b': (0.0, 0.1),
     'L0_ffn_norm2_w': (1.0, 0.6),
     'L0_ffn_norm2_b': (0.0, 0.55),
     'L0_ffn_b1': (0.0, 0.729),
     'L0_ffn_b2': (0.0, 0.1)}
    factors = {'L0_tok_pos_emb': 2.727, 'L0_attn_W_qkv': 3.602, 'L0_ffn_qkv_w': 4.023}
    for name, (base, spread) in spreads.items():
        noise = np.random.default_rng([zlib.crc32(name.encode()), seed]).standard_normal(out[name].shape)
        drawn = base * np.exp(spread * noise) if base else spread * noise
        out[name] = jnp.asarray(drawn.astype(out[name].dtype))
    for name, factor in factors.items():
        out[name] = (out[name] * factor).astype(out[name].dtype)
    return out
```

```python
from contextlib import ExitStack

import concourse.bass as bass
from concourse import mybir

F32 = mybir.dt.float32
F32R = mybir.dt.float32r
ALU = mybir.AluOpType
ACT = mybir.ActivationFunctionType
AX_X = mybir.AxisListType.X

P = 128
T, D = 1024, 192
TILES = T // P
GROUPS = 2
GT = TILES // GROUPS
GN = GT * P
TAIL = D - P
HEADS, HD = 12, 16
SEQ = 16
QUAD = 32
NQ = P // QUAD
HG = HEADS // NQ
KP = 768 // P
EXPERTS, HID = 8, 768
HC = HID // P
PADN = 256
QKC = 2 * HG
VAUG = HD + 1
EPS = 1e-5
SCALES = (float(D) ** -0.5, float(HD) ** -0.5)
PAIR = 2
W_QKV = QKC * P + PADN
RAW = 2 * HID + HC * D
LAG = 2


def front_order():
    order = [("tok", 0), ("tok", 1)]
    for n in range(2):
        order += [("turn", 2 * n, 0), ("turn", 2 * n, 1), ("qkv", n, 0), ("qkv", n, 1)]
        order += [("score", n, 0), ("flip", n, 0), ("score", n, 1), ("mix", n, 0), ("flip", n, 1), ("norm", n, 0),
                  ("score", n, 2), ("mix", n, 1), ("flip", n, 2), ("norm", n, 1), ("score", n, 3),
                  ("turn", 2 * n + 1, 0), ("mix", n, 2), ("proj", n, 0), ("flip", n, 3), ("norm", n, 2), ("mix", n, 3),
                  ("norm", n, 3), ("turn", 2 * n + 1, 1), ("proj", n, 1)]
    order += [("turn", 4, 0), ("turn", 4, 1), ("gate", 0), ("gate", 1), ("gsum", 0), ("gsum", 1)]
    return order


ORDER = front_order()


def ring_uses():
    uses = {}
    for stage in ORDER:
        kind = stage[0]
        if kind == "qkv":
            _, n, g = stage
            keys = [("qk", n, g, c) for c in range(QKC)] + [("v", n, g, p) for p in range(2)]
        elif kind in ("tok", "gate", "gsum"):
            keys = [(kind, stage[1], p) for p in range(2)]
        elif kind == "proj":
            keys = [("proj", stage[1], stage[2], p) for p in range(2)]
        else:
            keys = []
        for key in keys:
            uses[key] = len(uses)
    return uses


RING = ring_uses()
TURNS = {stage: u for u, stage in enumerate(
    [s for s in ORDER if s[0] == "turn"] + [("gate", 0), ("gate", 1)])}


def vit_moe_kernel(nc, xT, tok_w, posb, wqkv, wout, qk_bias, rows, cols, consts, w_exp, b1, b2, out):
    with ExitStack() as ctx:
        def sb(name, shape, dt=F32):
            return ctx.enter_context(nc.sbuf_tensor(name, shape, dt))

        def sem(name):
            return ctx.enter_context(nc.semaphore(name))

        early = sb("early", [P, GROUPS * KP * GN])
        patches = early[:, :].rearrange("p (g c n) -> p g c n", g=GROUPS, c=KP)
        raw_e = early[:, 0:2 * RAW].rearrange("p (s r) -> p s r", s=2)
        tokw = sb("tokw", [P, KP, D])
        pos = sb("pos", [P, 2, D])
        rowsb = sb("rowsb", [P, 4, D])
        qkb = sb("qkb", [P, 2, QKC])
        col = sb("col", [P, 2, 2, 2])
        const = sb("const", [P, P + QUAD + 64])
        ident = const[:, 0:P]
        other_image = const[:, P:P + QUAD]
        lower = const[:, P + QUAD:P + QUAD + 64].rearrange("p (e j) -> p e j", e=EXPERTS)
        wide_hi = sb("wide_hi", [P, 4 * W_QKV], F32R)
        wide_lo = sb("wide_lo", [P, 4 * W_QKV], F32R)
        qkv_hi, qkv_lo = (w[:, :].rearrange("p (n m c) -> p n m c", n=2, m=2) for w in (wide_hi, wide_lo))
        w1_hi, w1_lo = (w[:, 0:4 * HID].rearrange("p (s c) -> p s c", s=2) for w in (wide_hi, wide_lo))
        out_hi = sb("out_hi", [P, 3, 2, PADN], F32R)
        out_lo = sb("out_lo", [P, 3, 2, PADN], F32R)
        b1c = sb("b1c", [P, EXPERTS, HC])
        b2r = sb("b2r", [EXPERTS, D])

        H = sb("H", [P, TILES, D])
        Y = sb("Y", [P, TILES, D])
        X = sb("X", [P, TILES, 2 * P])
        R = sb("R", [P, TILES, D])
        bn = sb("bn", [P, TILES, 6])
        mv = sb("mv", [P, TILES, 2])
        var_eps = sb("var_eps", [P, TILES])
        minus_half = sb("minus_half", [P, TILES])
        rstd = sb("rstd", [P, TILES])
        xt32 = sb("xt32", [P, GROUPS, 2, GN])
        xt_hi = sb("xt_hi", [P, GROUPS, GN], F32R)
        xt_lo = sb("xt_lo", [P, GROUPS, GN], F32R)
        xt_tail = sb("xt_tail", [P, GROUPS, GN], F32R)
        late = sb("late", [P, GROUPS * QKC * GN])
        qkT = late[:, :].rearrange("p (g c n) -> p g c n", g=GROUPS, c=QKC)
        raw_small = [late[:, 0:2 * W_QKV].rearrange("p (m c) -> p m c", m=2),
                     early[:, RAW:RAW + 2 * W_QKV].rearrange("p (m c) -> p m c", m=2)]
        raw_out = late[:, QKC * GN:QKC * GN + 6 * PADN].rearrange("p (w m c) -> p w m c", w=3, m=2)
        V = sb("V", [P, TILES, HEADS, VAUG])
        SC = PAIR * HEADS * QUAD
        S = sb("S", [P, 2, SC])
        St = sb("St", [P, 2, SC])
        rowmax = sb("rowmax", [P, 2, PAIR * HEADS])
        rden = sb("rden", [P, 2, PAIR * HEADS])
        L = sb("L", [P, TILES, EXPERTS])
        Lx = sb("Lx", [P, TILES, EXPERTS])
        top = sb("top", [P, TILES])
        beats, ties = (S[:, b, 0:GT * EXPERTS * EXPERTS].rearrange("p (t e j) -> p t e j", t=GT, e=EXPERTS)
                       for b in range(2))
        rank = sb("rank", [P, TILES, EXPERTS])
        gates = sb("gates", [P, TILES, EXPERTS])
        gsum = sb("gsum", [P, TILES])
        gatesT = sb("gatesT", [EXPERTS, GROUPS, GN])
        w2s = sb("w2s", [P, 2, HC, 2 * D], F32R)
        NH = 4
        hid32 = late[:, 0:NH * GN].rearrange("p (k n) -> p k n", k=NH)
        hid_hi = sb("hid_hi", [P, NH, GN], F32R)
        hid_lo = sb("hid_lo", [P, NH, GN], F32R)

        psum = ctx.enter_context(nc.psum_tensor("psum", [P, 8, 512], F32))

        ld_tok, ld_x0, ld_x1, ld_small, ld_out, ld_misc = (sem(n) for n in (
            "ld_tok", "ld_x0", "ld_x1", "ld_small", "ld_out", "ld_misc"))
        ld_e = [sem("ld_e0"), sem("ld_e1")]
        ring_full = sem("ring_full")
        ring_free = [sem("ring_free0"), sem("ring_free1")]
        turn_full, turn_free, turn_32, xt_ready = sem("turn_full"), sem("turn_free"), sem("turn_32"), sem("xt_ready")
        o_ready = sem("o_ready")
        x_ready, var_ready, rstd_ready, setup = sem("x_ready"), sem("var_ready"), sem("rstd_ready"), sem("setup")
        small_hi, small_lo = sem("small_hi"), sem("small_lo")
        rows_done = sem("rows_done")
        score_full, score_free, shifted, exped, flipped = (sem(n) for n in (
            "score_full", "score_free", "shifted", "exped", "flipped"))
        mix_full, mix_free, dve_chain, act_chain = sem("mix_full"), sem("mix_free"), sem("dve_chain"), sem("act_chain")
        logit_shifted, logit_exped, gates_ready, gatesT_ready = (sem(n) for n in (
            "logit_shifted", "logit_exped", "gates_ready", "gatesT_ready"))
        base_ready = sem("base_ready")
        exp_hi, exp_lo = sem("exp_hi"), sem("exp_lo")
        up_full, up_free, hid_act, hid_ready, hid_used = (sem(n) for n in (
            "up_full", "up_free", "hid_act", "hid_ready", "hid_used"))
        down_full, down_free, stored = sem("down_full"), sem("down_free"), sem("stored")

        def ring_bank(key):
            return psum[:, 2 + RING[key] % 2, :]

        def pair_view(bank, width):
            return bank.rearrange("p (t c) -> p t c", t=2)[:, :, 0:width]

        def score_banks():
            return psum[:, 4:6, 0:PAIR * HG * QUAD * 2].rearrange("p b (r t g j) -> p b r t g j", r=2, t=PAIR, g=HG)

        block = ctx.enter_context(nc.Block())

        @block.sync
        def _(sp):
            sp.dma_start(tokw[:, :, :], tok_w).then_inc(ld_tok, 16)
            sp.dma_start(patches[:, 0, :, :], xT[:, 0]).then_inc(ld_x0, 16)
            sp.dma_start(pos[:, :, :], posb).then_inc(ld_misc, 16)
            sp.dma_start(const[:, :], consts).then_inc(ld_misc, 16)
            sp.dma_start(rowsb[:, :, :], rows).then_inc(ld_misc, 16)
            sp.dma_start(qkb[:, :, :], qk_bias).then_inc(ld_misc, 16)
            sp.dma_start(col[:, :, :, :], cols).then_inc(ld_misc, 16)
            sp.dma_start(raw_small[0], wqkv[0]).then_inc(ld_small, 16)
            sp.dma_start(patches[:, 1, :, :], xT[:, 1]).then_inc(ld_x1, 16)
            sp.dma_start(raw_out, wout).then_inc(ld_out, 16)
            sp.dma_start(b1c[:, :, :], b1).then_inc(ld_misc, 16)
            sp.dma_start(b2r[:, :], b2).then_inc(ld_misc, 16)
            sp.wait_ge(ring_full, RING[("tok", 1, 1)] + 1)
            sp.dma_start(raw_small[1], wqkv[1]).then_inc(ld_small, 16)
            for e in range(EXPERTS):
                if e == 1:
                    sp.wait_ge(small_lo, 3)
                if e >= 2:
                    sp.wait_ge(exp_lo, e - 1)
                sp.dma_start(raw_e[:, e % 2, :], w_exp[e]).then_inc(ld_e[e % 2], 16)
            for t in range(TILES):
                sp.wait_ge(down_free, (EXPERTS * GROUPS - GROUPS) * GT + t + 1)
                sp.dma_start(out[t], R[:, t, :]).then_inc(stored, 16)
            sp.wait_ge(stored, 16 * TILES)

        LD_MISC = 16 * 7

        def split_expert_lo(pool, e):
            s = e % 2
            pool.wait_ge(exp_hi, 2 * e + 2)
            nc.gpsimd.tensor_tensor(w1_lo[:, s, :], raw_e[:, s, 0:2 * HID], w1_hi[:, s, :].bitcast(F32), ALU.subtract)
            w2 = raw_e[:, s, 2 * HID:RAW].rearrange("p (c d) -> p c d", c=HC)
            nc.gpsimd.tensor_tensor(w2s[:, s, :, D:2 * D], w2, w2s[:, s, :, 0:D].bitcast(F32), ALU.subtract) \
                .then_inc(exp_lo, 1)

        @block.gpsimd
        def _(pool):
            nc.gpsimd.memset(minus_half[:, :], -0.5).then_inc(setup, 1)
            nc.gpsimd.memset(V[:, :, :, HD:VAUG], 1.0).then_inc(setup, 1)
            pool.wait_ge(setup, 2)
            norms = 0

            def root():
                nonlocal norms
                g = NORM_GROUPS[norms]
                pool.wait_ge(var_ready, norms + 1)
                s = slice(g * GT, g * GT + GT)
                nc.gpsimd.tensor_tensor(rstd[:, s], var_eps[:, s], minus_half[:, s], ALU.pow).then_inc(rstd_ready, 1)
                norms += 1

            def split_small(n):
                pool.wait_ge(small_hi, (1, 3)[n])
                nc.gpsimd.tensor_tensor(qkv_lo[:, n, :, :], raw_small[n], qkv_hi[:, n, :, :].bitcast(F32),
                                        ALU.subtract).then_inc(small_lo, 1)

            NORM_GROUPS = []
            for stage in ORDER:
                NORM_GROUPS += {"tok": [stage[1]], "proj": ([stage[-1]] * (2 - stage[1]))}.get(stage[0], [])
            split_small(0)
            for stage in ORDER:
                if stage[0] == "tok":
                    root()
                elif stage[0] == "proj":
                    for _ in range(2 - stage[1]):
                        root()
                elif stage == ("turn", 0, 0):
                    pool.wait_ge(small_hi, 2)
                    nc.gpsimd.tensor_tensor(out_lo[:, :, :, :], raw_out, out_hi[:, :, :, :].bitcast(F32),
                                            ALU.subtract).then_inc(small_lo, 1)
                elif stage == ("score", 0, 1):
                    split_small(1)
                elif stage == ("score", 1, 1):
                    split_expert_lo(pool, 0)
            for e in range(1, EXPERTS):
                split_expert_lo(pool, e)

        def split_expert_hi(act, e):
            s = e % 2
            act.wait_ge(ld_e[s], 16 * (e // 2 + 1))
            if e >= 2:
                act.wait_ge(down_full, (e - 1) * GROUPS * GT)
            nc.scalar.activation(w1_hi[:, s, :], raw_e[:, s, 0:2 * HID], ACT.Copy).then_inc(exp_hi, 1)
            w2 = raw_e[:, s, 2 * HID:RAW].rearrange("p (c d) -> p c d", c=HC)
            nc.scalar.activation(w2s[:, s, :, 0:D], w2, ACT.Copy).then_inc(exp_hi, 1)

        def chunk_used(eng, j):
            if j % HC == HC - 1:
                eng.wait_ge(down_full, (j // HC + 1) * GT)
            else:
                eng.wait_ge(hid_used, j // HC * (HC - 1) + j % HC + 1)

        @block.scalar
        def _(act):
            act.wait_ge(ld_small, 16)
            nc.scalar.activation(qkv_hi[:, 0, :, :], raw_small[0], ACT.Copy).then_inc(small_hi, 1)
            act.wait_ge(ld_out, 16)
            nc.scalar.activation(out_hi[:, :, :, :], raw_out, ACT.Copy).then_inc(small_hi, 1)
            act.wait_ge(ld_misc, LD_MISC)
            for stage in ORDER:
                kind = stage[0]
                if kind == "turn":
                    _, j, g = stage
                    u = TURNS[stage]
                    act.wait_ge(turn_full, u + 1)
                    if j in (2, 4):
                        affine = [dict(scale=col[:, j // 2 - 1, 0, m:m + 1], bias=col[:, j // 2 - 1, 1, m:m + 1])
                                  for m in range(2)]
                    else:
                        affine = [{}, {}]
                    func = ACT.Identity if j in (2, 4) else ACT.Copy
                    for m, hi in enumerate((xt_hi, xt_tail)):
                        nc.scalar.activation(xt32[:, g, m, :], psum[:, m, :], func, **affine[m]).then_inc(turn_32, 1)
                        nc.scalar.activation(hi[:, g, :], psum[:, m, :], func, **affine[m]).then_inc(
                            turn_free if m else turn_32, 1)
                elif kind == "qkv":
                    _, n, g = stage
                    act.wait_ge(small_lo, g + 1)
                    for c in range(QKC):
                        key = ("qk", n, g, c)
                        act.wait_ge(ring_full, RING[key] + 1)
                        nc.scalar.activation(qkT[:, g, c, :], ring_bank(key), ACT.Identity,
                                             bias=qkb[:, n, c:c + 1]).then_inc(ring_free[RING[key] % 2], 1)
                elif kind == "score":
                    _, n, p = stage
                    s = 4 * n + p
                    act.wait_ge(shifted, s + 1)
                    nc.scalar.activation(S[:, s % 2, :], S[:, s % 2, :], ACT.Exp, scale=SCALES[n]).then_inc(exped, 1)
                    if (n, p) == (0, 0):
                        act.wait_ge(ld_small, 32)
                        nc.scalar.activation(qkv_hi[:, 1, :, :], raw_small[1], ACT.Copy).then_inc(small_hi, 1)
                    if (n, p) == (1, 0):
                        split_expert_hi(act, 0)
                elif kind == "gate":
                    g = stage[1]
                    s = slice(g * GT, g * GT + GT)
                    act.wait_ge(logit_shifted, g + 1)
                    nc.scalar.activation(Lx[:, s, :], Lx[:, s, :], ACT.Exp).then_inc(logit_exped, 1)
                    act.wait_ge(turn_full, TURNS[stage] + 1)
                    nc.scalar.activation(gatesT[:, g, :], psum[0:EXPERTS, 0, :], ACT.Copy).then_inc(turn_free, 1)
            for k in range(EXPERTS * GROUPS * HC):
                e, g, c = k // (GROUPS * HC), k // HC % GROUPS, k % HC
                act.wait_ge(up_full, k + 1)
                if k >= NH:
                    chunk_used(act, k - NH)
                else:
                    act.wait_ge(base_ready, 1)
                bias = b1c[:, e, c:c + 1]
                nc.scalar.activation(hid32[:, k % NH, :], psum[:, k % 2, :], ACT.Gelu, bias=bias).then_inc(hid_act, 1)
                nc.scalar.activation(hid_hi[:, k % NH, :], psum[:, k % 2, :], ACT.Gelu, bias=bias).then_inc(up_free, 1)
                if k % (GROUPS * HC) == LAG + 2 and e + 1 < EXPERTS:
                    split_expert_hi(act, e + 1)

        @block.vector
        def _(dve):
            chain = 0

            def link(ins):
                nonlocal chain
                chain += 1
                ins.then_inc(dve_chain, 1)
                dve.wait_ge(dve_chain, chain)

            norms = 0

            def layernorm(src, dst, g, last):
                nonlocal norms
                tiles = range(g * GT, g * GT + GT)
                for t in tiles:
                    ins = nc.vector.bn_stats(bn[:, t, :], src[:, t, :])
                link(ins)
                for t in tiles:
                    ins = nc.vector.bn_aggr(mv[:, t, :], bn[:, t, :])
                link(ins)
                s = slice(g * GT, g * GT + GT)
                nc.vector.tensor_scalar(var_eps[:, s], mv[:, s, 1], EPS, None, ALU.add).then_inc(var_ready, 1)
                norms += 1
                dve.wait_ge(rstd_ready, norms)
                for t in tiles:
                    ins = nc.vector.tensor_scalar(dst[:, t, 0:D], src[:, t, :], mv[:, t, 0:1], rstd[:, t:t + 1],
                                                  ALU.subtract, ALU.mult)
                link(ins)
                if last:
                    tail_twice(s).then_inc(x_ready, 1)

            def tail_twice(s):
                return nc.vector.tensor_copy(X[:, s, D:2 * P], X[:, s, P:D])

            def add_row(dst, row, g):
                s = slice(g * GT, g * GT + GT)
                link(nc.vector.tensor_tensor(dst[:, s, :], dst[:, s, :], row.unsqueeze(1).to_broadcast([P, GT, D]),
                                             ALU.add))

            dve.wait_ge(ld_misc, LD_MISC)
            link(nc.vector.tensor_tensor(pos[:, 0, :], pos[:, 0, :], pos[:, 1, :], ALU.add))
            dve.wait_ge(setup, 2)
            for stage in ORDER:
                kind = stage[0]
                if kind == "tok":
                    g = stage[1]
                    for p in range(2):
                        key = ("tok", g, p)
                        t = g * GT + p * 2
                        dve.wait_ge(ring_full, RING[key] + 1)
                        ins = nc.vector.tensor_tensor(H[:, t:t + 2, :], pair_view(ring_bank(key), D),
                                                      pos[:, 0:1, :].to_broadcast([P, 2, D]), ALU.add)
                        ins.then_inc(ring_free[RING[key] % 2], 1)
                        dve.wait_ge(ring_free[RING[key] % 2], RING[key] // 2 + 1)
                    layernorm(H, X, g, True)
                elif kind == "turn":
                    _, j, g = stage
                    u = TURNS[stage]
                    dve.wait_ge(turn_32, 3 * u + 3)
                    nc.vector.tensor_tensor(xt_lo[:, g, :], xt32[:, g, 0, :], xt_hi[:, g, :].bitcast(F32), ALU.subtract)
                    dve.wait_ge(turn_free, u + 1)
                    nc.vector.tensor_tensor(xt_tail[TAIL:P, g, :], xt32[TAIL:P, g, 1, :],
                                            xt_tail[TAIL:P, g, :].bitcast(F32), ALU.subtract).then_inc(xt_ready, 1)
                elif kind == "qkv":
                    _, n, g = stage
                    for p in range(2):
                        key = ("v", n, g, p)
                        dve.wait_ge(ring_full, RING[key] + 1)
                        for i in range(2):
                            t = g * GT + 2 * p + i
                            src = pair_view(ring_bank(key), D)[:, i, :].rearrange("p (h d) -> p h d", h=HEADS)
                            bias = rowsb[:, 2 * n, :].rearrange("p (h d) -> p h d", h=HEADS)
                            ins = nc.vector.tensor_tensor(V[:, t, :, 0:HD], src, bias, ALU.add)
                        ins.then_inc(ring_free[RING[key] % 2], 1)
                elif kind == "score":
                    _, n, p = stage
                    s = 4 * n + p
                    b = s % 2
                    dve.wait_ge(score_full, s + 1)
                    banks = psum[:, 4:6, 0:SC // 2].rearrange("p b (x j) -> p b x j", j=QUAD)
                    mask = other_image.unsqueeze(1).unsqueeze(1).to_broadcast([P, 2, SC // 2 // QUAD, QUAD])
                    Sv = S[:, b, :].rearrange("p (b x j) -> p b x j", b=2, j=QUAD)
                    nc.vector.tensor_tensor(Sv, banks, mask, ALU.add).then_inc(score_free, 1)
                    dve.wait_ge(score_free, s + 1)
                    Sr = S[:, b, :].rearrange("p (x j) -> p x j", j=QUAD)
                    link(nc.vector.tensor_reduce(rowmax[:, b, :], Sr, AX_X, ALU.max))
                    nc.vector.tensor_tensor(Sr, Sr, rowmax[:, b, :].unsqueeze(2).to_broadcast([P, PAIR * HEADS, QUAD]),
                                            ALU.subtract).then_inc(shifted, 1)
                elif kind == "flip":
                    _, n, p = stage
                    s = 4 * n + p
                    dve.wait_ge(exped, s + 1)
                    nc.vector.transpose(St[:, s % 2, :], S[:, s % 2, :]).then_inc(flipped, 1)
                elif kind == "norm":
                    _, n, p = stage
                    s = 4 * n + p
                    dve.wait_ge(mix_full, s + 1)
                    mixed = psum[:, 6 + s % 2, 0:PAIR * HEADS * VAUG].rearrange("p (x d) -> p x d", d=VAUG)
                    link(nc.vector.reciprocal(rden[:, s % 2, :].unsqueeze(2), mixed[:, :, HD:VAUG]))
                    Xv = X[:, 2 * p:2 * p + 2, 0:D].rearrange("p t (h d) -> p t h d", h=HEADS)
                    mix = mixed[:, :, 0:HD].rearrange("p (t h) d -> p t h d", t=PAIR)
                    scale = rden[:, s % 2, :].rearrange("p (t h) -> p t h", t=PAIR).unsqueeze(3)
                    ins = nc.vector.tensor_tensor(Xv, mix, scale.to_broadcast([P, PAIR, HEADS, HD]), ALU.mult)
                    ins.then_inc(mix_free, 1)
                    dve.wait_ge(mix_free, s + 1)
                    tail_twice(slice(2 * p, 2 * p + 2)).then_inc(o_ready, 1)
                elif kind == "proj":
                    _, n, g = stage
                    res = (H, Y)[n]
                    for p in range(2):
                        key = ("proj", n, g, p)
                        t = g * GT + 2 * p
                        dve.wait_ge(ring_full, RING[key] + 1)
                        nc.vector.tensor_tensor(res[:, t:t + 2, :], pair_view(ring_bank(key), D), res[:, t:t + 2, :],
                                                ALU.add).then_inc(ring_free[RING[key] % 2], 1)
                        dve.wait_ge(ring_free[RING[key] % 2], RING[key] // 2 + 1)
                    add_row(res, rowsb[:, 2 * n + 1, :], g)
                    if n == 0:
                        layernorm(H, Y, g, False)
                        layernorm(Y, X, g, True)
                    else:
                        layernorm(Y, X, g, True)
                        s = slice(g * GT, g * GT + GT)
                        link(nc.vector.tensor_tensor(R[:, s, :], H[:, s, :], Y[:, s, :], ALU.add))
                elif kind == "gate":
                    g = stage[1]
                    s = slice(g * GT, g * GT + GT)
                    for p in range(2):
                        key = ("gate", g, p)
                        t = g * GT + 2 * p
                        dve.wait_ge(ring_full, RING[key] + 1)
                        nc.vector.tensor_copy(L[:, t:t + 2, :], pair_view(ring_bank(key), EXPERTS)) \
                            .then_inc(ring_free[RING[key] % 2], 1)
                        dve.wait_ge(ring_free[RING[key] % 2], RING[key] // 2 + 1)
                    link(nc.vector.tensor_reduce(top[:, s], L[:, s, :], AX_X, ALU.max))
                    nc.vector.tensor_tensor(Lx[:, s, :], L[:, s, :], top[:, s].unsqueeze(2).to_broadcast([P, GT, EXPERTS]),
                                            ALU.subtract).then_inc(logit_shifted, 1)
                    them = L[:, s, :].unsqueeze(2).to_broadcast([P, GT, EXPERTS, EXPERTS])
                    me = L[:, s, :].unsqueeze(3).to_broadcast([P, GT, EXPERTS, EXPERTS])
                    link(nc.vector.tensor_tensor(ties, them, me, ALU.is_equal))
                    link(nc.vector.tensor_tensor(ties, ties,
                                                 lower.unsqueeze(1).to_broadcast([P, GT, EXPERTS, EXPERTS]), ALU.mult))
                    link(nc.vector.tensor_tensor(beats, them, me, ALU.is_gt))
                    link(nc.vector.tensor_tensor(beats, beats, ties, ALU.add))
                    link(nc.vector.tensor_reduce(rank[:, s, :], beats, AX_X, ALU.add))
                    link(nc.vector.tensor_scalar(rank[:, s, :], rank[:, s, :], 1.5, None, ALU.is_lt))
                    dve.wait_ge(logit_exped, g + 1)
                    link(nc.vector.tensor_tensor(gates[:, s, :], rank[:, s, :], Lx[:, s, :], ALU.mult))
                    link(nc.vector.tensor_reduce(gsum[:, s], gates[:, s, :], AX_X, ALU.add))
                    link(nc.vector.reciprocal(gsum[:, s], gsum[:, s]))
                    nc.vector.tensor_tensor(gates[:, s, :], gates[:, s, :],
                                            gsum[:, s].unsqueeze(2).to_broadcast([P, GT, EXPERTS]),
                                            ALU.mult).then_inc(gates_ready, 1)
                elif kind == "gsum":
                    g = stage[1]
                    for p in range(2):
                        key = ("gsum", g, p)
                        t = g * GT + 2 * p
                        dve.wait_ge(ring_full, RING[key] + 1)
                        nc.vector.tensor_tensor(R[:, t:t + 2, :], pair_view(ring_bank(key), D), R[:, t:t + 2, :],
                                                ALU.add).then_inc(base_ready if (g, p) == (1, 1) else ring_free[RING[key] % 2], 1)
            dve.wait_ge(base_ready, 1)
            added = 0

            def add_expert(e, g):
                nonlocal added, chain
                wait_for = {}

                def part(i, m):
                    t = g * GT + i
                    u = (e * GROUPS + g) * GT + i
                    acc = psum[:, 2 + u % 6, m * D:m * D + D]
                    return nc.vector.scalar_tensor_tensor(R[:, t, :], acc, gates[:, t, e:e + 1], R[:, t, :],
                                                          ALU.mult, ALU.add)

                for i, m in ((0, 0), (1, 0), (0, 1), (2, 0), (1, 1), (3, 0), (2, 1), (3, 1)):
                    if m == 0:
                        dve.wait_ge(down_full, (e * GROUPS + g) * GT + i + 1)
                        chain += 1
                        wait_for[i] = chain
                        part(i, m).then_inc(dve_chain, 1)
                    else:
                        dve.wait_ge(dve_chain, wait_for[i])
                        part(i, m).then_inc(down_free, 1)
                added += 1
                dve.wait_ge(down_free, added * GT)

            steps = EXPERTS * GROUPS * HC
            for k in range(steps + LAG):
                if k < steps:
                    dve.wait_ge(up_free, k + 1)
                    dve.wait_ge(hid_act, k + 1)
                    nc.vector.tensor_tensor(hid_lo[:, k % NH, :], hid32[:, k % NH, :],
                                            hid_hi[:, k % NH, :].bitcast(F32), ALU.subtract).then_inc(hid_ready, 1)
                if k >= LAG and (k - LAG) % HC == HC - 1:
                    j = (k - LAG) // HC
                    add_expert(j // GROUPS, j % GROUPS)

        @block.tensor
        def _(pe):
            def take_ring(key):
                m = RING[key]
                if m >= 2:
                    pe.wait_ge(ring_free[m % 2], m // 2)
                return ring_bank(key)

            def take_turn(u):
                if u:
                    pe.wait_ge(turn_free, u)

            def project(key, g, p, w_hi, w_lo):
                bank = take_ring(key)
                for i in range(2):
                    o = bank[:, i * PADN:(i + 1) * PADN]
                    s = slice((2 * p + i) * P, (2 * p + i + 1) * P)
                    terms = [(xt_hi, w_hi[:, 0, :]), (xt_lo, w_hi[:, 0, :]), (xt_hi, w_lo[:, 0, :]),
                             (xt_tail, w_hi[:, 1, :]), (xt_tail, w_lo[:, 1, :])]
                    for j, (x, w) in enumerate(terms):
                        ins = nc.tensor.matmul(o, x[:, g, s], w, start=(j == 0), stop=(j == 4))
                ins.then_inc(ring_full, 1)

            pe.wait_ge(ld_tok, 16)
            for stage in ORDER:
                kind = stage[0]
                if kind == "tok":
                    g = stage[1]
                    pe.wait_ge((ld_x0, ld_x1)[g], 16)
                    for p in range(2):
                        key = ("tok", g, p)
                        bank = take_ring(key)
                        for i in range(2):
                            s = slice((2 * p + i) * P, (2 * p + i + 1) * P)
                            for c in range(KP):
                                ins = nc.tensor.matmul(bank[:, i * PADN:i * PADN + D], patches[:, g, c, s],
                                                       tokw[:, c, :], start=(c == 0), stop=(c == KP - 1))
                        ins.then_inc(ring_full, 1)
                elif kind == "turn":
                    _, j, g = stage
                    take_turn(TURNS[stage])
                    if j == 0 and g == 0:
                        pe.wait_ge(ld_misc, LD_MISC)
                    for i in range(GT):
                        t = g * GT + i
                        if j % 2 == 0:
                            pe.wait_ge(x_ready, j + g + 1)
                        else:
                            pe.wait_ge(o_ready, 4 * (j // 2) + 2 * g + i // 2 + 1)
                        nc.tensor.transpose(psum[:, 0, i * P:(i + 1) * P], X[:, t, 0:P], ident)
                        ins = nc.tensor.transpose(psum[:, 1, i * P:(i + 1) * P], X[:, t, P:2 * P], ident)
                    ins.then_inc(turn_full, 1)
                elif kind == "qkv":
                    _, n, g = stage
                    pe.wait_ge(xt_ready, TURNS[("turn", 2 * n, g)] + 1)
                    pe.wait_ge(small_lo, (1, 3)[n])
                    for c in range(QKC):
                        key = ("qk", n, g, c)
                        bank = take_ring(key)
                        s = slice(c * P, (c + 1) * P)
                        terms = [(qkv_hi[:, n, 0, s], xt_hi), (qkv_hi[:, n, 0, s], xt_lo), (qkv_lo[:, n, 0, s], xt_hi),
                                 (qkv_hi[:, n, 1, s], xt_tail), (qkv_lo[:, n, 1, s], xt_tail)]
                        for j, (w, x) in enumerate(terms):
                            ins = nc.tensor.matmul(bank, w, x[:, g, :], start=(j == 0), stop=(j == 4))
                        ins.then_inc(ring_full, 1)
                    s = slice(QKC * P, W_QKV)
                    for p in range(2):
                        project(("v", n, g, p), g, p, qkv_hi[:, n, :, s], qkv_lo[:, n, :, s])
                elif kind == "score":
                    _, n, p = stage
                    s = 4 * n + p
                    g = p // 2
                    last = RING[("v", n, g, 1)]
                    for b in range(2):
                        m = last - (last - b) % 2
                        pe.wait_ge(ring_free[b], m // 2 + 1)
                    if s:
                        pe.wait_ge(score_free, s)
                    banks = score_banks()
                    for r in range(NQ):
                        rows = slice(r * QUAD, r * QUAD + HD)
                        if r >= 2:
                            pe.wait_ge(rows_done, 2 * s + r - 1)
                        for i in range(PAIR):
                            for hg in range(HG):
                                for a in range(NQ):
                                    tok = (2 * p + i) % GT * P + a * QUAD
                                    ins = nc.tensor.matmul(
                                        banks[a * QUAD:(a + 1) * QUAD, r % 2, r // 2, i, hg, :],
                                        qkT[rows, g, hg, tok:tok + QUAD], qkT[rows, g, HG + hg, tok:tok + QUAD],
                                        start=True, stop=True, tile_position=(r * QUAD, a * QUAD))
                        if r < 2:
                            ins.then_inc(rows_done, 1)
                    ins.then_inc(score_full, 1)
                elif kind == "mix":
                    _, n, p = stage
                    s = 4 * n + p
                    pe.wait_ge(flipped, s + 1)
                    if s >= 2:
                        pe.wait_ge(mix_free, s - 1)
                    probs = St[:, s % 2, :].rearrange("p (b r t g i) -> p b r t g i", b=2, r=2, t=PAIR, g=HG)
                    for a in range(NQ):
                        q = slice(a * QUAD, (a + 1) * QUAD)
                        o = psum[q, 6 + s % 2, 0:PAIR * HEADS * VAUG].rearrange("p (t h d) -> p t h d", t=PAIR, h=HEADS)
                        for i in range(PAIR):
                            for h in range(HEADS):
                                r, hg = h % NQ, h // NQ
                                ins = nc.tensor.matmul(o[:, i, h, :], probs[q, r % 2, r // 2, i, hg, :],
                                                       V[q, 2 * p + i, h, :], start=True, stop=True,
                                                       tile_position=(a * QUAD, a * QUAD))
                    ins.then_inc(mix_full, 1)
                elif kind == "proj":
                    _, n, g = stage
                    pe.wait_ge(xt_ready, TURNS[("turn", 2 * n + 1, g)] + 1)
                    pe.wait_ge(small_lo, 2)
                    for p in range(2):
                        project(("proj", n, g, p), g, p, out_hi[:, n], out_lo[:, n])
                elif kind == "gate":
                    g = stage[1]
                    pe.wait_ge(xt_ready, TURNS[("turn", 4, g)] + 1)
                    for p in range(2):
                        project(("gate", g, p), g, p, out_hi[:, 2], out_lo[:, 2])
                    pe.wait_ge(gates_ready, g + 1)
                    take_turn(TURNS[stage])
                    for i in range(GT):
                        ins = nc.tensor.transpose(psum[0:EXPERTS, 0, i * P:(i + 1) * P], gates[:, g * GT + i, :], ident)
                    ins.then_inc(turn_full, 1)
                elif kind == "gsum":
                    g = stage[1]
                    pe.wait_ge(turn_free, TURNS[("gate", g)] + 1)
                    for p in range(2):
                        key = ("gsum", g, p)
                        bank = take_ring(key)
                        for i in range(2):
                            s = slice((2 * p + i) * P, (2 * p + i + 1) * P)
                            ins = nc.tensor.matmul(bank[:, i * PADN:i * PADN + D], gatesT[:, g, s], b2r[:, :],
                                                   start=True, stop=True)
                        ins.then_inc(ring_full, 1)

            pe.wait_ge(base_ready, 1)
            steps = EXPERTS * GROUPS * HC
            for k in range(steps + LAG):
                if k < steps:
                    e, g, c = k // (GROUPS * HC), k // HC % GROUPS, k % HC
                    w = e % 2
                    if k % (GROUPS * HC) == 0:
                        pe.wait_ge(exp_lo, e + 1)
                    if k >= 2:
                        pe.wait_ge(up_free, k - 1)
                    m, tl = slice(c * P, (c + 1) * P), slice(HID + c * P, HID + (c + 1) * P)
                    terms = [(w1_hi[:, w, m], xt_hi), (w1_hi[:, w, m], xt_lo), (w1_lo[:, w, m], xt_hi),
                             (w1_hi[:, w, tl], xt_tail), (w1_lo[:, w, tl], xt_tail)]
                    for j, (wt, x) in enumerate(terms):
                        ins = nc.tensor.matmul(psum[:, k % 2, :], wt, x[:, g, :], start=(j == 0), stop=(j == 4))
                    ins.then_inc(up_full, 1)
                if k >= LAG:
                    j = k - LAG
                    e, g, c = j // (GROUPS * HC), j // HC % GROUPS, j % HC
                    w = e % 2
                    pe.wait_ge(hid_ready, j + 1)
                    for i in range(GT):
                        u = (e * GROUPS + g) * GT + i
                        if c == 0 and u >= 6:
                            pe.wait_ge(down_free, u - 5)
                        s = slice(i * P, (i + 1) * P)
                        acc = psum[:, 2 + u % 6, :]
                        nc.tensor.matmul(acc[:, 0:PADN], hid_lo[:, j % NH, s], w2s[:, w, c, 0:PADN],
                                         start=(c == 0), stop=(c == HC - 1))
                        ins = nc.tensor.matmul(acc[:, 0:2 * D], hid_hi[:, j % NH, s], w2s[:, w, c, :],
                                               start=False, stop=(c == HC - 1), skip_group_check=True)
                        if c == HC - 1:
                            ins.then_inc(down_full, 1)
                    if c < HC - 1:
                        ins.then_inc(hid_used, 1)


def kernel(**inputs):
    import numpy as np
    import concourse.bacc as bacc
    from concourse import mybir as mb
    from concourse.bass_utils import run_bass_kernel_spmd

    a = {k: np.asarray(v) for k, v in inputs.items()}
    f = np.float32

    def main_tail(w, width):
        o = np.zeros((P, 2, width), f)
        o[:, 0, :w.shape[1]] = w[0:P]
        o[0:TAIL, 1, :w.shape[1]] = w[P:D]
        o[TAIL:P, 1, :w.shape[1]] = w[P:D]
        return o

    def spread(w, axis_rows):
        o = np.zeros((axis_rows, 2, HG, NQ, QUAD), f)
        o[..., 0:HD] = w.reshape(axis_rows, 2, HG, NQ, HD)
        return o.reshape(axis_rows, QKC * P)

    wq = a["L0_attn_W_qkv"].reshape(HEADS, HD, 3, HD)
    dense = np.zeros((HEADS, HD, 3, HEADS, HD), f)
    for h in range(HEADS):
        dense[h, :, :, h, :] = wq[h]
    qkv = [dense.reshape(D, 3 * D), a["L0_ffn_qkv_w"].T]
    bias = [a["L0_attn_b_qkv"].reshape(HEADS, 3, HD).transpose(1, 0, 2).reshape(1, 3 * D),
            a["L0_ffn_qkv_b"].reshape(1, 3 * D)]
    wqkv = np.stack([main_tail(np.concatenate([spread(w[:, 0:2 * D], D), w[:, 2 * D:]], 1), W_QKV) for w in qkv])
    qk_bias = np.stack([spread(b[:, 0:2 * D], 1).reshape(QKC, P).T for b in bias], 1)
    wout = np.stack([main_tail(w, PADN) for w in (a["L0_attn_W_out"], a["L0_ffn_proj_w"].T, a["L0_ffn_w_gate"])], 1)
    rows = np.stack([bias[0][0, 2 * D:], a["L0_attn_b_out"], bias[1][0, 2 * D:], a["L0_ffn_proj_b"]])
    rows = np.broadcast_to(rows, (P, 4, D))
    posb = np.stack([np.tile(a["L0_tok_pos_emb"], (P // SEQ, 1)), np.broadcast_to(a["L0_tok_b"], (P, D))], 1)
    cols = np.stack([np.stack([np.stack([v[0:P], np.concatenate([v[P:D], v[P:D]])], 1)
                               for v in (a[f"L0_ffn_{m}_w"], a[f"L0_ffn_{m}_b"])], 1) for m in ("norm1", "norm2")], 1)
    patches = a["x"].reshape(64, 4, 16, 4, 16, 3).transpose(0, 1, 3, 2, 4, 5).reshape(GROUPS, GN, KP, P)
    w1 = a["L0_ffn_W1"]
    w_exp = np.concatenate([w1[:, 0:P], np.concatenate([w1[:, P:D], w1[:, P:D]], 1),
                            a["L0_ffn_W2"].reshape(EXPERTS, HC, P, D).transpose(0, 2, 1, 3).reshape(EXPERTS, P, HC * D)], 2)
    i, j = np.arange(P)[:, None], np.arange(QUAD)[None, :]
    other = np.where(i % QUAD // SEQ == j // SEQ, 0.0, -1e30)
    lower = np.broadcast_to(np.arange(EXPERTS)[None, :] < np.arange(EXPERTS)[:, None], (P, EXPERTS, EXPERTS))
    arrays = {
        "xT": patches.transpose(3, 0, 2, 1), "tok_w": a["L0_tok_W"].reshape(KP, P, D).transpose(1, 0, 2),
        "posb": posb, "wqkv": wqkv, "wout": wout, "qk_bias": qk_bias, "rows": rows, "cols": cols,
        "consts": np.concatenate([np.eye(P), other, lower.reshape(P, -1)], 1).astype(f),
        "w_exp": w_exp, "b1": a["L0_ffn_b1"].reshape(EXPERTS, HC, P).transpose(2, 0, 1), "b2": a["L0_ffn_b2"],
    }
    arrays = {f"in_{k}": np.ascontiguousarray(v) for k, v in arrays.items()}
    nc = bacc.Bacc("TRN2", target_bir_lowering=False, num_devices=1)
    args = [nc.dram_tensor(k, v.shape, mb.dt.from_np(v.dtype), kind="ExternalInput").ap() for k, v in arrays.items()]
    args.append(nc.dram_tensor("out_0", (TILES, P, D), mb.dt.float32, kind="ExternalOutput").ap())
    vit_moe_kernel(nc, *args)
    r = run_bass_kernel_spmd(nc, [arrays], core_ids=[0])
    return r.results[0]["out_0"].reshape(64, SEQ, D)
```

```python
from contextlib import ExitStack

import concourse.bass as bass
from concourse import mybir

F32 = mybir.dt.float32
F32R = mybir.dt.float32r
ALU = mybir.AluOpType
ACT = mybir.ActivationFunctionType
AX_X = mybir.AxisListType.X

P = 128
T, D = 1024, 192
TILES = T // P
GROUPS = 2
GT = TILES // GROUPS
GN = GT * P
TAIL = D - P
HEADS, HD = 12, 16
SEQ = 16
QUAD = 32
NQ = P // QUAD
HG = HEADS // NQ
KP = 768 // P
EXPERTS, HID = 8, 768
HC = HID // P
PADN = 256
QKC = 2 * HG
VAUG = HD + 1
EPS = 1e-5
SCALES = (float(D) ** -0.5, float(HD) ** -0.5)
PAIR = 2
W_QKV = QKC * P + PADN
RAW = 2 * HID + HC * D
SPLIT_AT = 4
LAG = 2


STEPS = EXPERTS * GROUPS * HC
EARLY = HC


def attention_order():
    blocks = [(n, g) for n in range(2) for g in range(2)]
    order = [("tok", 0), ("turn", 0, 0), ("tok", 1), ("qkv", 0, 0)]
    for b, (n, g) in enumerate(blocks):
        p = 2 * g
        before = blocks[b - 1] if b else None
        after = blocks[b + 1] if b + 1 < len(blocks) else None
        order += [("score", n, p), ("flip", n, p)]
        if before:
            order += [("turn", 2 * before[0] + 1, before[1])]
        order += [("score", n, p + 1)]
        if before:
            order += [("proj",) + before]
        order += [("mix", n, p), ("flip", n, p + 1), ("norm", n, p)]
        if after:
            order += [("turn", 2 * after[0], after[1]), ("qkv",) + after]
        else:
            order += [("turn", 4, 0), ("gate", 0)]
        order += [("mix", n, p + 1), ("norm", n, p + 1)]
    return order


def whole_order():
    order = attention_order()
    order += [("up", 0), ("turn", 3, 1), ("up", 1), ("up", 2), ("proj", 1, 1), ("down", 0), ("up", 3),
              ("gates", 0), ("down", 1), ("up", 4), ("down", 2), ("up", 5), ("down", 3), ("turn", 4, 1), ("down", 4),
              ("gate", 1), ("down", 5), ("add", 0, (0, 1)), ("add", 0, (2, 3)), ("gates", 1)]
    for k in range(EARLY, STEPS + LAG):
        if k < STEPS:
            order += [("up", k)]
        j = k - LAG
        if j < EARLY or (j % HC == 0 and k < STEPS):
            continue
        order += [("down", j - 1), ("down", j)] if j % HC == 1 else [("down", j)]
        if j % HC == HC - 1:
            order += [("add", j // HC, (0, 1))]
        if j % HC == 1 and j > EARLY + 1:
            order += [("add", j // HC - 1, (2, 3))]
    order += [("add", EXPERTS * GROUPS - 1, (2, 3))]
    return order


ORDER = whole_order()


def ring_uses():
    uses = {}
    for stage in ORDER:
        kind = stage[0]
        if kind == "qkv":
            _, n, g = stage
            keys = [("qk", n, g, c) for c in range(QKC)] + [("v", n, g, p) for p in range(2)]
        elif kind in ("tok", "gate", "gates"):
            keys = [(kind, stage[1], p) for p in range(2)]
        elif kind == "up":
            keys = [stage]
        elif kind == "proj":
            keys = [("proj", stage[1], stage[2], p) for p in range(2)]
        else:
            keys = []
        for key in keys:
            uses[key] = len(uses)
    return uses


RING = ring_uses()
TURNS = {stage: u for u, stage in enumerate(s for s in ORDER if s[0] in ("turn", "gates"))}
XT = {stage[1:]: u for u, stage in enumerate(s for s in ORDER if s[0] == "turn")}
ACC_BANKS = (4, 5, 6, 7, 0, 1)


def vit_moe_kernel(nc, xT, tok_w, posb, wqkv, wout, qk_bias, rows, cols, consts, w_exp, b1, b2, out):
    with ExitStack() as ctx:
        def sb(name, shape, dt=F32):
            return ctx.enter_context(nc.sbuf_tensor(name, shape, dt))

        def sem(name):
            return ctx.enter_context(nc.semaphore(name))

        early = sb("early", [P, TILES * KP * P])
        patches = early[:, :].rearrange("p (t c n) -> p t c n", t=TILES, c=KP)
        raw_e = early[:, 0:2 * RAW].rearrange("p (s r) -> p s r", s=2)
        tokw = sb("tokw", [P, KP, D])
        pos = sb("pos", [P, 2, D])
        rowsb = sb("rowsb", [P, 4, D])
        qkb = sb("qkb", [P, 2, QKC])
        col = sb("col", [P, 2, 2, 2])
        const = sb("const", [P, P + QUAD + 64])
        ident = const[:, 0:P]
        other_image = const[:, P:P + QUAD]
        lower = const[:, P + QUAD:P + QUAD + 64].rearrange("p (e j) -> p e j", e=EXPERTS)
        wide_hi = sb("wide_hi", [P, 4 * W_QKV], F32R)
        wide_lo = sb("wide_lo", [P, 4 * W_QKV], F32R)
        qkv_hi, qkv_lo = (w[:, :].rearrange("p (n m c) -> p n m c", n=2, m=2) for w in (wide_hi, wide_lo))
        w1_hi, w1_lo = (w[:, 0:4 * HID].rearrange("p (s c) -> p s c", s=2) for w in (wide_hi, wide_lo))
        out_hi = sb("out_hi", [P, 3, 2, PADN], F32R)
        out_lo = sb("out_lo", [P, 3, 2, PADN], F32R)
        b1c = sb("b1c", [P, EXPERTS, HC])
        b2r = sb("b2r", [EXPERTS, D])

        H = sb("H", [P, TILES, D])
        Y = sb("Y", [P, TILES, D])
        X = sb("X", [P, TILES, 2 * P])
        R = sb("R", [P, TILES, D])
        bn = sb("bn", [P, TILES, 6])
        mv = sb("mv", [P, TILES, 2])
        var_eps = sb("var_eps", [P, GROUPS, 2, GT])
        minus_half = sb("minus_half", [P, 2, GT])
        rstd = sb("rstd", [P, GROUPS, 2, GT])
        xt32 = sb("xt32", [P, GROUPS, 2, GN])
        xt_hi = sb("xt_hi", [P, GROUPS, GN], F32R)
        xt_lo = sb("xt_lo", [P, GROUPS, GN], F32R)
        xt_tail = sb("xt_tail", [P, GROUPS, GN], F32R)
        late = sb("late", [P, GROUPS * QKC * GN])
        qkT = late[:, :].rearrange("p (g c n) -> p g c n", g=GROUPS, c=QKC)
        raw_small = [late[:, 0:2 * W_QKV].rearrange("p (m c) -> p m c", m=2),
                     early[:, RAW:RAW + 2 * W_QKV].rearrange("p (m c) -> p m c", m=2)]
        raw_out = late[:, QKC * GN:QKC * GN + 6 * PADN].rearrange("p (w m c) -> p w m c", w=3, m=2)
        V = sb("V", [P, TILES, HEADS, VAUG])
        SC = PAIR * HEADS * QUAD
        S = sb("S", [P, 2, SC])
        St = sb("St", [P, 2, SC])
        rowmax = sb("rowmax", [P, 2, PAIR * HEADS])
        rden = sb("rden", [P, 2, PAIR * HEADS])
        L = sb("L", [P, TILES, EXPERTS])
        Lx = sb("Lx", [P, TILES, EXPERTS])
        top = sb("top", [P, TILES])
        beats, ties = (S[:, b, 0:GT * EXPERTS * EXPERTS].rearrange("p (t e j) -> p t e j", t=GT, e=EXPERTS)
                       for b in range(2))
        rank = sb("rank", [P, TILES, EXPERTS])
        gates = sb("gates", [P, TILES, EXPERTS])
        gsum = sb("gsum", [P, TILES])
        gatesT = sb("gatesT", [EXPERTS, GROUPS, GN])
        w2s = sb("w2s", [P, 2, HC, 2 * D], F32R)
        NH = 4
        hid32 = late[:, 0:NH * GN].rearrange("p (k n) -> p k n", k=NH)
        hid_hi = sb("hid_hi", [P, NH, GN], F32R)
        hid_lo = sb("hid_lo", [P, NH, GN], F32R)

        psum = ctx.enter_context(nc.psum_tensor("psum", [P, 8, 512], F32))

        ld_tok, ld_small, ld_out, ld_misc = (sem(n) for n in ("ld_tok", "ld_small", "ld_out", "ld_misc"))
        ld_x = [sem(f"ld_x{p}") for p in range(TILES // PAIR)]
        ld_e = [sem("ld_e0"), sem("ld_e1")]
        ring_full = sem("ring_full")
        ring_free = [sem("ring_free0"), sem("ring_free1")]
        turn_full, turn_free, turn_hi, tail_out, xt_ready = (sem(n) for n in (
            "turn_full", "turn_free", "turn_hi", "tail_out", "xt_ready"))
        o_ready = sem("o_ready")
        x_ready, var_ready, rstd_ready, setup = sem("x_ready"), sem("var_ready"), sem("rstd_ready"), sem("setup")
        small_hi, small_lo = sem("small_hi"), sem("small_lo")
        rows_done = sem("rows_done")
        score_full, score_free, shifted, exped, flipped = (sem(n) for n in (
            "score_full", "score_free", "shifted", "exped", "flipped"))
        mix_full, mix_free, dve_chain, act_chain = sem("mix_full"), sem("mix_free"), sem("dve_chain"), sem("act_chain")
        logit_shifted, logit_exped, gates_ready, gatesT_ready = (sem(n) for n in (
            "logit_shifted", "logit_exped", "gates_ready", "gatesT_ready"))
        exp_hi, exp_lo = sem("exp_hi"), sem("exp_lo")
        hid_act, hid_ready, hid_used = (sem(n) for n in ("hid_act", "hid_ready", "hid_used"))
        down_full, down_free, stored = sem("down_full"), sem("down_free"), sem("stored")

        def ring_bank(key):
            return psum[:, 2 + RING[key] % 2, :]

        def pair_view(bank, width):
            return bank.rearrange("p (t c) -> p t c", t=2)[:, :, 0:width]

        def ring_read(eng, key):
            eng.wait_ge(ring_free[RING[key] % 2], RING[key] // 2 + 1)

        block = ctx.enter_context(nc.Block())

        @block.sync
        def _(sp):
            def load_patches(p):
                sp.dma_start(patches[:, 2 * p:2 * p + 2], xT[:, 2 * p:2 * p + 2]).then_inc(ld_x[p], 16)

            load_patches(0)
            load_patches(1)
            sp.dma_start(rowsb[:, :, :], rows).then_inc(ld_misc, 16)
            sp.dma_start(qkb[:, :, :], qk_bias).then_inc(ld_misc, 16)
            sp.dma_start(col[:, :, :, :], cols).then_inc(ld_misc, 16)
            sp.dma_start(raw_small[0], wqkv[0]).then_inc(ld_small, 16)
            load_patches(2)
            load_patches(3)
            sp.dma_start(raw_out, wout).then_inc(ld_out, 16)
            sp.dma_start(b1c[:, :, :], b1).then_inc(ld_misc, 16)
            sp.dma_start(b2r[:, :], b2).then_inc(ld_misc, 16)
            sp.wait_ge(ring_full, RING[("tok", 1, 1)] + 1)
            sp.dma_start(raw_small[1], wqkv[1]).then_inc(ld_small, 16)
            for e in range(EXPERTS):
                if e == 1:
                    sp.wait_ge(small_lo, 3)
                if e >= 2:
                    sp.wait_ge(exp_lo, e - 1)
                sp.dma_start(raw_e[:, e % 2, :], w_exp[e]).then_inc(ld_e[e % 2], 16)
            for t in range(TILES):
                sp.wait_ge(down_free, (EXPERTS * GROUPS - GROUPS) * GT + t + 1)
                sp.dma_start(out[t], R[:, t, :]).then_inc(stored, 16)
            sp.wait_ge(stored, 16 * TILES)

        LD_MISC = 16 * 7

        def split_expert_lo(pool, e):
            s = e % 2
            pool.wait_ge(exp_hi, 2 * e + 2)
            nc.gpsimd.tensor_tensor(w1_lo[:, s, :], raw_e[:, s, 0:2 * HID], w1_hi[:, s, :].bitcast(F32), ALU.subtract)
            w2 = raw_e[:, s, 2 * HID:RAW].rearrange("p (c d) -> p c d", c=HC)
            nc.gpsimd.tensor_tensor(w2s[:, s, :, D:2 * D], w2, w2s[:, s, :, 0:D].bitcast(F32), ALU.subtract) \
                .then_inc(exp_lo, 1)

        @block.gpsimd
        def _(pool):
            nc.gpsimd.memset(minus_half[:, :, :], -0.5).then_inc(setup, 1)
            nc.gpsimd.memset(V[:, :, :, HD:VAUG], 1.0).then_inc(setup, 1)
            pool.wait_ge(setup, 2)
            norms = 0

            def root(g, twice):
                nonlocal norms
                norms += 1
                pool.wait_ge(var_ready, norms)
                m = 2 if twice else 1
                nc.gpsimd.tensor_tensor(rstd[:, g, 0:m], var_eps[:, g, 0:m], minus_half[:, 0:m], ALU.pow) \
                    .then_inc(rstd_ready, 1)

            def split_small(n):
                pool.wait_ge(small_hi, (1, 3)[n])
                nc.gpsimd.tensor_tensor(qkv_lo[:, n, :, :], raw_small[n], qkv_hi[:, n, :, :].bitcast(F32),
                                        ALU.subtract).then_inc(small_lo, 1)

            split_small(0)
            for stage in ORDER:
                if stage[0] == "tok":
                    root(stage[1], False)
                elif stage[0] == "proj":
                    root(stage[2], stage[1] == 0)
                    if stage == ("proj", 1, 0):
                        split_expert_lo(pool, 0)
                elif stage == ("turn", 0, 0):
                    pool.wait_ge(small_hi, 2)
                    nc.gpsimd.tensor_tensor(out_lo[:, :, :, :], raw_out, out_hi[:, :, :, :].bitcast(F32),
                                            ALU.subtract).then_inc(small_lo, 1)
                elif stage == ("score", 0, 1):
                    split_small(1)
                elif stage[0] == "up" and stage[1] % (GROUPS * HC) == SPLIT_AT:
                    if stage[1] // (GROUPS * HC) + 1 < EXPERTS:
                        split_expert_lo(pool, stage[1] // (GROUPS * HC) + 1)

        def split_expert_hi(act, e):
            s = e % 2
            act.wait_ge(ld_e[s], 16 * (e // 2 + 1))
            if e >= 2:
                act.wait_ge(down_full, (e - 1) * GROUPS * GT)
            nc.scalar.activation(w1_hi[:, s, :], raw_e[:, s, 0:2 * HID], ACT.Copy).then_inc(exp_hi, 1)
            w2 = raw_e[:, s, 2 * HID:RAW].rearrange("p (c d) -> p c d", c=HC)
            nc.scalar.activation(w2s[:, s, :, 0:D], w2, ACT.Copy).then_inc(exp_hi, 1)

        def chunk_used(eng, j):
            if j % HC == HC - 1:
                eng.wait_ge(down_full, (j // HC + 1) * GT)
            else:
                eng.wait_ge(hid_used, j // HC * (HC - 1) + j % HC + 1)

        @block.scalar
        def _(act):
            act.dma_start(tokw[:, :, :], tok_w).then_inc(ld_tok, 16)
            act.dma_start(pos[:, :, :], posb).then_inc(ld_misc, 16)
            act.dma_start(const[:, :], consts).then_inc(ld_misc, 16)
            act.wait_ge(ld_small, 16)
            nc.scalar.activation(qkv_hi[:, 0, :, :], raw_small[0], ACT.Copy).then_inc(small_hi, 1)
            act.wait_ge(ld_out, 16)
            nc.scalar.activation(out_hi[:, :, :, :], raw_out, ACT.Copy).then_inc(small_hi, 1)
            act.wait_ge(ld_misc, LD_MISC)
            for stage in ORDER:
                kind = stage[0]
                if kind == "turn":
                    _, j, g = stage
                    u = TURNS[stage]
                    act.wait_ge(turn_full, u + 1)
                    for m, hi in enumerate((xt_hi, xt_tail)):
                        if m:
                            act.wait_ge(tail_out, XT[j, g] + 1)
                        if j in (2, 4):
                            scale, bias = (col[:, j // 2 - 1, v, m:m + 1] for v in range(2))
                            ins = nc.scalar.activation(hi[:, g, :], psum[:, m, :], ACT.Identity, scale=scale, bias=bias)
                        else:
                            ins = nc.scalar.activation(hi[:, g, :], psum[:, m, :], ACT.Copy)
                        ins.then_inc(turn_hi, 1)
                elif kind == "qkv":
                    _, n, g = stage
                    act.wait_ge(small_lo, g + 1)
                    for c in range(QKC):
                        key = ("qk", n, g, c)
                        act.wait_ge(ring_full, RING[key] + 1)
                        nc.scalar.activation(qkT[:, g, c, :], ring_bank(key), ACT.Identity,
                                             bias=qkb[:, n, c:c + 1]).then_inc(ring_free[RING[key] % 2], 1)
                elif kind == "score":
                    _, n, p = stage
                    s = 4 * n + p
                    act.wait_ge(shifted, s + 1)
                    nc.scalar.activation(S[:, s % 2, :], S[:, s % 2, :], ACT.Exp, scale=SCALES[n]).then_inc(exped, 1)
                    if (n, p) == (0, 0):
                        act.wait_ge(ld_small, 32)
                        nc.scalar.activation(qkv_hi[:, 1, :, :], raw_small[1], ACT.Copy).then_inc(small_hi, 1)
                    if (n, p) == (1, 2):
                        act.wait_ge(ring_full, RING[("v", 1, 1, 1)] + 1)
                        split_expert_hi(act, 0)
                elif kind == "gate":
                    g = stage[1]
                    s = slice(g * GT, g * GT + GT)
                    act.wait_ge(logit_shifted, g + 1)
                    nc.scalar.activation(Lx[:, s, :], Lx[:, s, :], ACT.Exp).then_inc(logit_exped, 1)
                elif kind == "gates":
                    g = stage[1]
                    act.wait_ge(turn_full, TURNS[stage] + 1)
                    nc.scalar.activation(gatesT[:, g, :], psum[0:EXPERTS, 0, :], ACT.Copy).then_inc(turn_free, 1)
                elif kind == "up":
                    k = stage[1]
                    e, c = k // (GROUPS * HC), k % HC
                    act.wait_ge(ring_full, RING[stage] + 1)
                    if k >= NH:
                        chunk_used(act, k - NH)
                    else:
                        act.wait_ge(score_full, 2 * TILES)
                    bias = b1c[:, e, c:c + 1]
                    nc.scalar.activation(hid32[:, k % NH, :], ring_bank(stage), ACT.Gelu, bias=bias).then_inc(hid_act, 1)
                    nc.scalar.activation(hid_hi[:, k % NH, :], ring_bank(stage), ACT.Gelu, bias=bias) \
                        .then_inc(ring_free[RING[stage] % 2], 1)
                    if k % (GROUPS * HC) == SPLIT_AT and e + 1 < EXPERTS:
                        split_expert_hi(act, e + 1)

        @block.vector
        def _(dve):
            chain = 0

            def link(ins):
                nonlocal chain
                chain += 1
                ins.then_inc(dve_chain, 1)
                dve.wait_ge(dve_chain, chain)

            norms = 0

            def moments(src, t):
                for i in (t, t + 1):
                    ins = nc.vector.bn_stats(bn[:, i, :], src[:, i, :])
                link(ins)
                for i in (t, t + 1):
                    ins = nc.vector.bn_aggr(mv[:, i, :], bn[:, i, :])
                return ins

            def scaled(src, dst, g, m):
                for i in range(GT):
                    t = g * GT + i
                    ins = nc.vector.tensor_scalar(dst[:, t, 0:D], src[:, t, :], mv[:, t, 0:1], rstd[:, g, m, i:i + 1],
                                                  ALU.subtract, ALU.mult)
                link(ins)

            def normalise(src, g, twice):
                nonlocal norms
                s = slice(g * GT, g * GT + GT)
                ins = nc.vector.tensor_scalar(var_eps[:, g, 0, :], mv[:, s, 1], EPS, None, ALU.add)
                if twice:
                    ins = nc.vector.tensor_scalar(var_eps[:, g, 1, :], mv[:, s, 1], 1 + EPS, EPS ** 2, ALU.mult, ALU.add)
                ins.then_inc(var_ready, 1)
                norms += 1
                dve.wait_ge(rstd_ready, norms)
                scaled(src, X, g, 1 if twice else 0)
                tail_twice(s).then_inc(x_ready, 1)

            def tail_twice(s):
                return nc.vector.tensor_copy(X[:, s, D:2 * P], X[:, s, P:D])

            def add_row(dst, row, g):
                s = slice(g * GT, g * GT + GT)
                link(nc.vector.tensor_tensor(dst[:, s, :], dst[:, s, :], row.unsqueeze(1).to_broadcast([P, GT, D]),
                                             ALU.add))

            dve.wait_ge(ld_misc, LD_MISC)
            link(nc.vector.tensor_tensor(pos[:, 0, :], pos[:, 0, :], pos[:, 1, :], ALU.add))
            dve.wait_ge(setup, 2)
            for stage in ORDER:
                kind = stage[0]
                if kind == "tok":
                    g = stage[1]
                    for p in range(2):
                        key = ("tok", g, p)
                        t = g * GT + p * 2
                        dve.wait_ge(ring_full, RING[key] + 1)
                        ins = nc.vector.tensor_tensor(H[:, t:t + 2, :], pair_view(ring_bank(key), D),
                                                      pos[:, 0:1, :].to_broadcast([P, 2, D]), ALU.add)
                        ins.then_inc(ring_free[RING[key] % 2], 1)
                        ring_read(dve, key)
                        link(moments(H, t))
                    normalise(H, g, False)
                    add_row(H, rowsb[:, 1, :], g)
                elif kind == "turn":
                    _, j, g = stage
                    dve.wait_ge(turn_full, TURNS[stage] + 1)
                    u = XT[j, g]

                    def full(m):
                        if j in (2, 4):
                            scale, bias = (col[:, j // 2 - 1, v, m:m + 1] for v in range(2))
                            return nc.vector.tensor_scalar(xt32[:, g, m, :], psum[:, m, :], scale, bias, ALU.mult, ALU.add)
                        return nc.vector.tensor_copy(xt32[:, g, m, :], psum[:, m, :])

                    full(1).then_inc(tail_out, 1)
                    dve.wait_ge(turn_hi, 2 * u + 1)
                    full(0).then_inc(turn_free, 1)
                    dve.wait_ge(turn_free, TURNS[stage] + 1)
                    nc.vector.tensor_tensor(xt_lo[:, g, :], xt32[:, g, 0, :], xt_hi[:, g, :].bitcast(F32),
                                            ALU.subtract)
                    dve.wait_ge(turn_hi, 2 * u + 2)
                    dve.wait_ge(tail_out, u + 1)
                    nc.vector.tensor_tensor(xt_tail[TAIL:P, g, :], xt32[TAIL:P, g, 1, :],
                                            xt_tail[TAIL:P, g, :].bitcast(F32), ALU.subtract).then_inc(xt_ready, 1)
                elif kind == "qkv":
                    _, n, g = stage
                    for p in range(2):
                        key = ("v", n, g, p)
                        dve.wait_ge(ring_full, RING[key] + 1)
                        for i in range(2):
                            t = g * GT + 2 * p + i
                            src = pair_view(ring_bank(key), D)[:, i, :].rearrange("p (h d) -> p h d", h=HEADS)
                            bias = rowsb[:, 2 * n, :].rearrange("p (h d) -> p h d", h=HEADS)
                            ins = nc.vector.tensor_tensor(V[:, t, :, 0:HD], src, bias, ALU.add)
                        ins.then_inc(ring_free[RING[key] % 2], 1)
                elif kind == "score":
                    _, n, p = stage
                    s = 4 * n + p
                    b = s % 2
                    for i in range(PAIR):
                        dve.wait_ge(score_full, PAIR * s + i + 1)
                        w = SC // PAIR
                        scores = psum[:, 4 + i, 0:w].rearrange("p (x j) -> p x j", j=QUAD)
                        mask = other_image.unsqueeze(1).to_broadcast([P, HEADS, QUAD])
                        nc.vector.tensor_tensor(S[:, b, i * w:(i + 1) * w].rearrange("p (x j) -> p x j", j=QUAD),
                                                scores, mask, ALU.add).then_inc(score_free, 1)
                    dve.wait_ge(score_free, PAIR * (s + 1))
                    Sr = S[:, b, :].rearrange("p (x j) -> p x j", j=QUAD)
                    link(nc.vector.tensor_reduce(rowmax[:, b, :], Sr, AX_X, ALU.max))
                    nc.vector.tensor_tensor(Sr, Sr, rowmax[:, b, :].unsqueeze(2).to_broadcast([P, PAIR * HEADS, QUAD]),
                                            ALU.subtract).then_inc(shifted, 1)
                elif kind == "flip":
                    _, n, p = stage
                    s = 4 * n + p
                    dve.wait_ge(exped, s + 1)
                    nc.vector.transpose(St[:, s % 2, :], S[:, s % 2, :]).then_inc(flipped, 1)
                elif kind == "norm":
                    _, n, p = stage
                    s = 4 * n + p
                    dve.wait_ge(mix_full, s + 1)
                    mixed = psum[:, 6 + s % 2, 0:PAIR * HEADS * VAUG].rearrange("p (x d) -> p x d", d=VAUG)
                    link(nc.vector.reciprocal(rden[:, s % 2, :].unsqueeze(2), mixed[:, :, HD:VAUG]))
                    Xv = X[:, 2 * p:2 * p + 2, 0:D].rearrange("p t (h d) -> p t h d", h=HEADS)
                    mix = mixed[:, :, 0:HD].rearrange("p (t h) d -> p t h d", t=PAIR)
                    scale = rden[:, s % 2, :].rearrange("p (t h) -> p t h", t=PAIR).unsqueeze(3)
                    ins = nc.vector.tensor_tensor(Xv, mix, scale.to_broadcast([P, PAIR, HEADS, HD]), ALU.mult)
                    ins.then_inc(mix_free, 1)
                    dve.wait_ge(mix_free, s + 1)
                    tail_twice(slice(2 * p, 2 * p + 2)).then_inc(o_ready, 1)
                elif kind == "proj":
                    _, n, g = stage
                    res = (H, Y)[n]
                    for p in range(2):
                        key = ("proj", n, g, p)
                        t = g * GT + 2 * p
                        dve.wait_ge(ring_full, RING[key] + 1)
                        nc.vector.tensor_tensor(res[:, t:t + 2, :], pair_view(ring_bank(key), D), res[:, t:t + 2, :],
                                                ALU.add).then_inc(ring_free[RING[key] % 2], 1)
                        ring_read(dve, key)
                        link(moments(res, t))
                    normalise(res, g, n == 0)
                    if n == 0:
                        scaled(H, Y, g, 0)
                    else:
                        s = slice(g * GT, g * GT + GT)
                        link(nc.vector.tensor_tensor(R[:, s, :], H[:, s, :], Y[:, s, :], ALU.add))
                    if n == 0:
                        add_row(Y, rowsb[:, 3, :], g)
                elif kind == "gate":
                    g = stage[1]
                    s = slice(g * GT, g * GT + GT)
                    for p in range(2):
                        key = ("gate", g, p)
                        t = g * GT + 2 * p
                        dve.wait_ge(ring_full, RING[key] + 1)
                        nc.vector.tensor_copy(L[:, t:t + 2, :], pair_view(ring_bank(key), EXPERTS)) \
                            .then_inc(ring_free[RING[key] % 2], 1)
                        dve.wait_ge(ring_free[RING[key] % 2], RING[key] // 2 + 1)
                    link(nc.vector.tensor_reduce(top[:, s], L[:, s, :], AX_X, ALU.max))
                    nc.vector.tensor_tensor(Lx[:, s, :], L[:, s, :], top[:, s].unsqueeze(2).to_broadcast([P, GT, EXPERTS]),
                                            ALU.subtract).then_inc(logit_shifted, 1)
                    them = L[:, s, :].unsqueeze(2).to_broadcast([P, GT, EXPERTS, EXPERTS])
                    me = L[:, s, :].unsqueeze(3).to_broadcast([P, GT, EXPERTS, EXPERTS])
                    link(nc.vector.tensor_tensor(ties, them, me, ALU.is_equal))
                    link(nc.vector.tensor_tensor(ties, ties,
                                                 lower.unsqueeze(1).to_broadcast([P, GT, EXPERTS, EXPERTS]), ALU.mult))
                    link(nc.vector.tensor_tensor(beats, them, me, ALU.is_gt))
                    link(nc.vector.tensor_tensor(beats, beats, ties, ALU.add))
                    link(nc.vector.tensor_reduce(rank[:, s, :], beats, AX_X, ALU.add))
                    link(nc.vector.tensor_scalar(rank[:, s, :], rank[:, s, :], 1.5, None, ALU.is_lt))
                    dve.wait_ge(logit_exped, g + 1)
                    link(nc.vector.tensor_tensor(gates[:, s, :], rank[:, s, :], Lx[:, s, :], ALU.mult))
                    link(nc.vector.tensor_reduce(gsum[:, s], gates[:, s, :], AX_X, ALU.add))
                    link(nc.vector.reciprocal(gsum[:, s], gsum[:, s]))
                    nc.vector.tensor_tensor(gates[:, s, :], gates[:, s, :],
                                            gsum[:, s].unsqueeze(2).to_broadcast([P, GT, EXPERTS]),
                                            ALU.mult).then_inc(gates_ready, 1)
                elif kind == "gates":
                    g = stage[1]
                    for p in range(2):
                        key = ("gates", g, p)
                        t = g * GT + 2 * p
                        dve.wait_ge(ring_full, RING[key] + 1)
                        nc.vector.tensor_tensor(R[:, t:t + 2, :], pair_view(ring_bank(key), D), R[:, t:t + 2, :],
                                                ALU.add).then_inc(ring_free[RING[key] % 2], 1)
                        ring_read(dve, key)
                elif kind == "up":
                    k = stage[1]
                    dve.wait_ge(hid_act, k + 1)
                    ring_read(dve, stage)
                    nc.vector.tensor_tensor(hid_lo[:, k % NH, :], hid32[:, k % NH, :],
                                            hid_hi[:, k % NH, :].bitcast(F32), ALU.subtract).then_inc(hid_ready, 1)
                elif kind == "add":
                    _, j, tiles = stage
                    e, g = j // GROUPS, j % GROUPS

                    def part(i, m):
                        t, u = g * GT + i, j * GT + i
                        acc = psum[:, ACC_BANKS[u % 6], m * D:m * D + D]
                        return nc.vector.scalar_tensor_tensor(R[:, t, :], acc, gates[:, t, e:e + 1], R[:, t, :],
                                                              ALU.mult, ALU.add)

                    if e:
                        dve.wait_ge(down_free, (j - GROUPS) * GT + tiles[-1] + 1)
                    first = chain
                    for i in tiles:
                        dve.wait_ge(down_full, j * GT + i + 1)
                        part(i, 0).then_inc(dve_chain, 1)
                        chain += 1
                    for n, i in enumerate(tiles):
                        dve.wait_ge(dve_chain, first + n + 1)
                        part(i, 1).then_inc(down_free, 1)

        @block.tensor
        def _(pe):
            def take_ring(key):
                m = RING[key]
                if m >= 2:
                    pe.wait_ge(ring_free[m % 2], m // 2)
                return ring_bank(key)

            def take_turn(stage):
                u = TURNS[stage]
                before = sum(TURNS[s] < u for s in TURNS if s[0] == "turn")
                if u:
                    pe.wait_ge(turn_free, u)
                if before:
                    pe.wait_ge(turn_hi, 2 * before)

            def project(key, g, p, w_hi, w_lo):
                bank = take_ring(key)
                for i in range(2):
                    o = bank[:, i * PADN:(i + 1) * PADN]
                    s = slice((2 * p + i) * P, (2 * p + i + 1) * P)
                    terms = [(xt_hi, w_hi[:, 0, :]), (xt_lo, w_hi[:, 0, :]), (xt_hi, w_lo[:, 0, :]),
                             (xt_tail, w_hi[:, 1, :]), (xt_tail, w_lo[:, 1, :])]
                    for j, (x, w) in enumerate(terms):
                        ins = nc.tensor.matmul(o, x[:, g, s], w, start=(j == 0), stop=(j == 4))
                ins.then_inc(ring_full, 1)

            pe.wait_ge(ld_tok, 16)
            for stage in ORDER:
                kind = stage[0]
                if kind == "tok":
                    g = stage[1]
                    for p in range(2):
                        pe.wait_ge(ld_x[2 * g + p], 16)
                        key = ("tok", g, p)
                        bank = take_ring(key)
                        for i in range(2):
                            for c in range(KP):
                                ins = nc.tensor.matmul(bank[:, i * PADN:i * PADN + D], patches[:, g * GT + 2 * p + i, c, :],
                                                       tokw[:, c, :], start=(c == 0), stop=(c == KP - 1))
                        ins.then_inc(ring_full, 1)
                elif kind == "turn":
                    _, j, g = stage
                    take_turn(stage)
                    if j == 0 and g == 0:
                        pe.wait_ge(ld_misc, LD_MISC)
                    for i in range(GT):
                        t = g * GT + i
                        if j % 2 == 0:
                            pe.wait_ge(x_ready, j + g + 1)
                        else:
                            pe.wait_ge(o_ready, 4 * (j // 2) + 2 * g + i // 2 + 1)
                        nc.tensor.transpose(psum[:, 0, i * P:(i + 1) * P], X[:, t, 0:P], ident)
                        ins = nc.tensor.transpose(psum[:, 1, i * P:(i + 1) * P], X[:, t, P:2 * P], ident)
                    ins.then_inc(turn_full, 1)
                elif kind == "qkv":
                    _, n, g = stage
                    pe.wait_ge(xt_ready, XT[2 * n, g] + 1)
                    pe.wait_ge(small_lo, (1, 3)[n])
                    for c in range(QKC):
                        key = ("qk", n, g, c)
                        bank = take_ring(key)
                        s = slice(c * P, (c + 1) * P)
                        terms = [(qkv_hi[:, n, 0, s], xt_hi), (qkv_hi[:, n, 0, s], xt_lo), (qkv_lo[:, n, 0, s], xt_hi),
                                 (qkv_hi[:, n, 1, s], xt_tail), (qkv_lo[:, n, 1, s], xt_tail)]
                        if n == 0:
                            terms = terms[:3] if c % HG < 2 else terms[3:]
                        for j, (w, x) in enumerate(terms):
                            ins = nc.tensor.matmul(bank, w, x[:, g, :], start=(j == 0), stop=(j == len(terms) - 1))
                        ins.then_inc(ring_full, 1)
                    s = slice(QKC * P, W_QKV)
                    for p in range(2):
                        project(("v", n, g, p), g, p, qkv_hi[:, n, :, s], qkv_lo[:, n, :, s])
                elif kind == "score":
                    _, n, p = stage
                    s = 4 * n + p
                    g = p // 2
                    ring_read(pe, ("v", n, g, 0))
                    ring_read(pe, ("v", n, g, 1))
                    for i in range(PAIR):
                        tile = PAIR * s + i
                        if tile >= 2:
                            pe.wait_ge(score_free, tile - 1)
                        bank = psum[:, 4 + i, 0:SC // PAIR].rearrange("p (r g j) -> p r g j", r=NQ, g=HG)
                        for turn in range(NQ):
                            for r in range(NQ):
                                if turn:
                                    pe.wait_ge(rows_done, tile * NQ * (NQ - 1) + (turn - 1) * NQ + (r + 1) % NQ + 1)
                                rows = slice(r * QUAD, r * QUAD + HD)
                                a = (r + turn) % NQ
                                tok = (2 * p + i) % GT * P + a * QUAD
                                for hg in range(HG):
                                    ins = nc.tensor.matmul(
                                        bank[a * QUAD:(a + 1) * QUAD, r, hg, :],
                                        qkT[rows, g, hg, tok:tok + QUAD], qkT[rows, g, HG + hg, tok:tok + QUAD],
                                        start=True, stop=True, tile_position=(r * QUAD, a * QUAD))
                                if turn < NQ - 1:
                                    ins.then_inc(rows_done, 1)
                        ins.then_inc(score_full, 1)
                elif kind == "mix":
                    _, n, p = stage
                    s = 4 * n + p
                    pe.wait_ge(flipped, s + 1)
                    if s >= 2:
                        pe.wait_ge(mix_free, s - 1)
                    probs = St[:, s % 2, :].rearrange("p (t r g i) -> p t r g i", t=PAIR, r=NQ, g=HG)
                    for a in range(NQ):
                        q = slice(a * QUAD, (a + 1) * QUAD)
                        o = psum[q, 6 + s % 2, 0:PAIR * HEADS * VAUG].rearrange("p (t h d) -> p t h d", t=PAIR, h=HEADS)
                        for i in range(PAIR):
                            for h in range(HEADS):
                                ins = nc.tensor.matmul(o[:, i, h, :], probs[q, i, h % NQ, h // NQ, :],
                                                       V[q, 2 * p + i, h, :], start=True, stop=True,
                                                       tile_position=(a * QUAD, a * QUAD))
                    ins.then_inc(mix_full, 1)
                elif kind == "proj":
                    _, n, g = stage
                    pe.wait_ge(xt_ready, XT[2 * n + 1, g] + 1)
                    pe.wait_ge(small_lo, 2)
                    for p in range(2):
                        project(("proj", n, g, p), g, p, out_hi[:, n], out_lo[:, n])
                elif kind == "gate":
                    g = stage[1]
                    pe.wait_ge(xt_ready, XT[4, g] + 1)
                    for p in range(2):
                        project(("gate", g, p), g, p, out_hi[:, 2], out_lo[:, 2])
                elif kind == "gates":
                    g = stage[1]
                    pe.wait_ge(gates_ready, g + 1)
                    take_turn(stage)
                    for i in range(GT):
                        ins = nc.tensor.transpose(psum[0:EXPERTS, 0, i * P:(i + 1) * P], gates[:, g * GT + i, :], ident)
                    ins.then_inc(turn_full, 1)
                    pe.wait_ge(turn_free, TURNS[("gates", g)] + 1)
                    for p in range(2):
                        key = ("gates", g, p)
                        bank = take_ring(key)
                        for i in range(2):
                            s = slice((2 * p + i) * P, (2 * p + i + 1) * P)
                            ins = nc.tensor.matmul(bank[:, i * PADN:i * PADN + D], gatesT[:, g, s], b2r[:, :],
                                                   start=True, stop=True)
                        ins.then_inc(ring_full, 1)
                elif kind == "up":
                    k = stage[1]
                    e, g, c = k // (GROUPS * HC), k // HC % GROUPS, k % HC
                    w = e % 2
                    if k % (GROUPS * HC) == 0:
                        pe.wait_ge(exp_lo, e + 1)
                    if e == 0 and c == 0:
                        pe.wait_ge(xt_ready, XT[4, g] + 1)
                    bank = take_ring(stage)
                    m, tl = slice(c * P, (c + 1) * P), slice(HID + c * P, HID + (c + 1) * P)
                    terms = [(w1_hi[:, w, m], xt_hi), (w1_hi[:, w, m], xt_lo), (w1_lo[:, w, m], xt_hi),
                             (w1_hi[:, w, tl], xt_tail), (w1_lo[:, w, tl], xt_tail)]
                    for j, (wt, x) in enumerate(terms):
                        ins = nc.tensor.matmul(bank, wt, x[:, g, :], start=(j == 0), stop=(j == 4))
                    ins.then_inc(ring_full, 1)
                elif kind == "down":
                    k = stage[1]
                    e, g, c = k // (GROUPS * HC), k // HC % GROUPS, k % HC
                    w = e % 2
                    pe.wait_ge(hid_ready, k + 1)
                    if k == 0:
                        pe.wait_ge(score_free, 2 * TILES)
                        pe.wait_ge(mix_free, TILES)
                    if k == HC:
                        pe.wait_ge(turn_free, len(TURNS))
                        pe.wait_ge(turn_hi, 2 * len(XT))
                    for i in range(GT):
                        u = (e * GROUPS + g) * GT + i
                        if c == 0 and u >= 6:
                            pe.wait_ge(down_free, u - 5)
                        s = slice(i * P, (i + 1) * P)
                        acc = psum[:, ACC_BANKS[u % 6], :]
                        nc.tensor.matmul(acc[:, 0:PADN], hid_lo[:, k % NH, s], w2s[:, w, c, 0:PADN],
                                         start=(c == 0), stop=(c == HC - 1))
                        ins = nc.tensor.matmul(acc[:, 0:2 * D], hid_hi[:, k % NH, s], w2s[:, w, c, :],
                                               start=False, stop=(c == HC - 1), skip_group_check=True)
                        if c == HC - 1:
                            ins.then_inc(down_full, 1)
                    if c < HC - 1:
                        ins.then_inc(hid_used, 1)


def kernel(**inputs):
    import numpy as np
    import concourse.bacc as bacc
    from concourse import mybir as mb
    from concourse.bass_utils import run_bass_kernel_spmd

    a = {k: np.asarray(v) for k, v in inputs.items()}
    f = np.float32

    def main_tail(w, width):
        o = np.zeros((P, 2, width), f)
        o[:, 0, :w.shape[1]] = w[0:P]
        o[0:TAIL, 1, :w.shape[1]] = w[P:D]
        o[TAIL:P, 1, :w.shape[1]] = w[P:D]
        return o

    def spread(w, axis_rows):
        o = np.zeros((axis_rows, 2, HG, NQ, QUAD), f)
        o[..., 0:HD] = w.reshape(axis_rows, 2, HG, NQ, HD)
        return o.reshape(axis_rows, QKC * P)

    wq = a["L0_attn_W_qkv"].reshape(HEADS, HD, 3, HD)
    dense = np.zeros((HEADS, HD, 3, HEADS, HD), f)
    for h in range(HEADS):
        dense[h, :, :, h, :] = wq[h]
    qkv = [dense.reshape(D, 3 * D), a["L0_ffn_qkv_w"].T]
    bias = [a["L0_attn_b_qkv"].reshape(HEADS, 3, HD).transpose(1, 0, 2).reshape(1, 3 * D),
            a["L0_ffn_qkv_b"].reshape(1, 3 * D)]
    wqkv = np.stack([main_tail(np.concatenate([spread(w[:, 0:2 * D], D), w[:, 2 * D:]], 1), W_QKV) for w in qkv])
    qk_bias = np.stack([spread(b[:, 0:2 * D], 1).reshape(QKC, P).T for b in bias], 1)
    wout = np.stack([main_tail(w, PADN) for w in (a["L0_attn_W_out"], a["L0_ffn_proj_w"].T, a["L0_ffn_w_gate"])], 1)
    rows = np.stack([bias[0][0, 2 * D:], a["L0_attn_b_out"], bias[1][0, 2 * D:], a["L0_ffn_proj_b"]])
    rows = np.broadcast_to(rows, (P, 4, D))
    posb = np.stack([np.tile(a["L0_tok_pos_emb"], (P // SEQ, 1)), np.broadcast_to(a["L0_tok_b"], (P, D))], 1)
    cols = np.stack([np.stack([np.stack([v[0:P], np.concatenate([v[P:D], v[P:D]])], 1)
                               for v in (a[f"L0_ffn_{m}_w"], a[f"L0_ffn_{m}_b"])], 1) for m in ("norm1", "norm2")], 1)
    patches = a["x"].reshape(64, 4, 16, 4, 16, 3).transpose(0, 1, 3, 2, 4, 5).reshape(TILES, P, KP, P)
    w1 = a["L0_ffn_W1"]
    w_exp = np.concatenate([w1[:, 0:P], np.concatenate([w1[:, P:D], w1[:, P:D]], 1),
                            a["L0_ffn_W2"].reshape(EXPERTS, HC, P, D).transpose(0, 2, 1, 3).reshape(EXPERTS, P, HC * D)], 2)
    i, j = np.arange(P)[:, None], np.arange(QUAD)[None, :]
    other = np.where(i % QUAD // SEQ == j // SEQ, 0.0, -1e30)
    lower = np.broadcast_to(np.arange(EXPERTS)[None, :] < np.arange(EXPERTS)[:, None], (P, EXPERTS, EXPERTS))
    arrays = {
        "xT": patches.transpose(3, 0, 2, 1), "tok_w": a["L0_tok_W"].reshape(KP, P, D).transpose(1, 0, 2),
        "posb": posb, "wqkv": wqkv, "wout": wout, "qk_bias": qk_bias, "rows": rows, "cols": cols,
        "consts": np.concatenate([np.eye(P), other, lower.reshape(P, -1)], 1).astype(f),
        "w_exp": w_exp, "b1": a["L0_ffn_b1"].reshape(EXPERTS, HC, P).transpose(2, 0, 1), "b2": a["L0_ffn_b2"],
    }
    arrays = {f"in_{k}": np.ascontiguousarray(v) for k, v in arrays.items()}
    nc = bacc.Bacc("TRN2", target_bir_lowering=False, num_devices=1)
    args = [nc.dram_tensor(k, v.shape, mb.dt.from_np(v.dtype), kind="ExternalInput").ap() for k, v in arrays.items()]
    args.append(nc.dram_tensor("out_0", (TILES, P, D), mb.dt.float32, kind="ExternalOutput").ap())
    vit_moe_kernel(nc, *args)
    r = run_bass_kernel_spmd(nc, [arrays], core_ids=[0])
    return r.results[0]["out_0"].reshape(64, SEQ, D)
```

```python
from contextlib import ExitStack

import concourse.bass as bass
from concourse import mybir

F32 = mybir.dt.float32
F32R = mybir.dt.float32r
ALU = mybir.AluOpType
ACT = mybir.ActivationFunctionType
AX_X = mybir.AxisListType.X

P = 128
T, D = 1024, 192
TILES = T // P
GROUPS = 2
GT = TILES // GROUPS
GN = GT * P
TAIL = D - P
HEADS, HD = 12, 16
SEQ = 16
QUAD = 32
NQ = P // QUAD
HG = HEADS // NQ
KP = 768 // P
EXPERTS, HID = 8, 768
HC = HID // P
PADN = 256
Q_CHUNK, K_CHUNK = (0, 0, 1), (2, 3, 4)
HALF = (0, 1, 0)
QKC = 5
VAUG = HD + 1
EPS = 1e-5
SCALES = (float(D) ** -0.5, float(HD) ** -0.5)
PAIR = 2
W_QKV = QKC * P + PADN
RAW = 2 * HID + HC * D
SPLIT_AT = 4
LAG = 2
STEPS = EXPERTS * GROUPS * HC

FRONT = """
    tok.0.0 tok.0.1 ln.0.0 tok.1.0 tok.1.1 turn.0.0 lift.0.0 ln.0.1 qk.0.0.0 qk.0.0.1 qk.0.0.2 qk.0.0.3
    qk.0.0.4 turn.0.1 lift.0.1 post.0.0 v.0.0.0 score.0.0 soft.0.0 high.1 score.0.1 qk.0.1.0 soft.0.1
    qk.0.1.1 score.0.2 flip.0.0 post.0.1 qk.0.1.2 v.0.0.1 v.0.1.0 qk.0.1.3 mix.0.0 score.0.3 soft.0.2 low.1
    soft.0.3 qk.0.1.4 v.0.1.1 mix.0.1 score.0.4 norm.0.0 flip.0.1 mix.0.2 mix.0.3 norm.0.1 score.0.5
    turn.1.0 lift.1.0 soft.0.4 soft.0.5 score.0.6 flip.0.2 proj.0.0.0 proj.0.0.1 ln.2.0 mix.0.4 score.0.7
    turn.2.0 lift.2.0 soft.0.6 soft.0.7 mix.0.5 post.2.0 flip.0.3 qk.1.0.0 qk.1.0.1 qk.1.0.2 norm.0.2
    mix.0.6 qk.1.0.3 mix.0.7 norm.0.3 qk.1.0.4 turn.1.1 lift.1.1 score.1.0 proj.0.1.0 score.1.1 soft.1.0
    soft.1.1 proj.0.1.1 ln.2.1 v.1.0.0 flip.1.0 score.1.2 soft.1.2 v.1.0.1 score.1.3 turn.2.1 lift.2.1
    mix.1.0 mix.1.1 soft.1.3 norm.1.0 post.2.1 qk.1.1.0 qk.1.1.1 flip.1.1 v.1.1.0 mix.1.2 qk.1.1.2 mix.1.3
    norm.1.1 qk.1.1.3 qk.1.1.4 turn.3.0 lift.3.0 score.1.4 v.1.1.1 proj.1.0.0 soft.1.4 high.2 score.1.5
    proj.1.0.1 ln.4.0 low.2 soft.1.5 flip.1.2 score.1.6 score.1.7 soft.1.6 turn.4.0 lift.4.0 soft.1.7
    mix.1.4 flip.1.3 mix.1.5 norm.1.2 gate.0 mix.1.6 up.0 mix.1.7 norm.1.3 up.1 turn.3.1 lift.3.1 up.2
    proj.1.1.0 proj.1.1.1 down.0 ln.4.1 up.3 post.4.0 down.1 gates.0 turn.4.1 lift.4.1 post.4.1 down.2
    down.3 up.4 high.3 low.3 up.5 down.4 gate.1 up.6 down.5 add.0.0 up.7 gates.1 up.8 down.6 up.9 down.7
    up.10 down.8 add.0.1 down.9 up.11
"""


def front_order():
    order = []
    for word in FRONT.split():
        kind, *numbers = word.split(".")
        numbers = [int(x) for x in numbers]
        if kind == "add":
            numbers[1] = (2 * numbers[1], 2 * numbers[1] + 1)
        order.append((kind, *numbers))
    return order


def expert_order():
    order = []
    for k in range(STEPS + LAG):
        if k < STEPS:
            order += [("up", k)]
            if k % (GROUPS * HC) == SPLIT_AT and k + GROUPS * HC < STEPS:
                order += [(part, k // (GROUPS * HC) + 3) for part in ("high", "low")]
        j = k - LAG
        if j < 0 or (j % HC == 0 and k < STEPS):
            continue
        order += [("down", j - 1), ("down", j)] if j % HC == 1 else [("down", j)]
        if j % HC == HC - 1:
            order += [("add", j // HC, (0, 1))]
        if j % HC == 1 and j > 1:
            order += [("add", j // HC - 1, (2, 3))]
    return order + [("add", EXPERTS * GROUPS - 1, (2, 3))]


def whole_order():
    front = front_order()
    return front + [stage for stage in expert_order() if stage not in front]


ORDER = whole_order()


def ring_uses():
    uses = {}
    for stage in ORDER:
        kind = stage[0]
        if kind in ("tok", "qk", "v", "proj", "up"):
            keys = [stage]
        elif kind in ("gate", "gates"):
            keys = [(kind, stage[1], p) for p in range(2)]
        else:
            keys = []
        for key in keys:
            uses[key] = len(uses)
    return uses


RING = ring_uses()
TURNS = {stage: u for u, stage in enumerate(s for s in ORDER if s[0] in ("turn", "gates"))}
LNS = {stage: u for u, stage in enumerate(s for s in ORDER if s[0] == "ln")}
XT = {stage[1:]: u for u, stage in enumerate(s for s in ORDER if s[0] == "turn")}
AFFINE = {stage: u for u, stage in enumerate(s for s in XT if s[0] in (2, 4))}
SCORE_BANKS = (4, 5, 6)
MIX_BANK = 7
ACC_BANKS = (4, 5, 6, 7, 0, 1)


def vit_moe_kernel(nc, xT, tok_w, posb, wqkv, wout, qk_bias, rows, cols, consts, w_exp, b1, b2, out):
    with ExitStack() as ctx:
        def sb(name, shape, dt=F32):
            return ctx.enter_context(nc.sbuf_tensor(name, shape, dt))

        def sem(name):
            return ctx.enter_context(nc.semaphore(name))

        early = sb("early", [P, TILES * KP * P])
        patches = early[:, :].rearrange("p (t c n) -> p t c n", t=TILES, c=KP)
        raw_e = early[:, 0:2 * RAW].rearrange("p (s r) -> p s r", s=2)
        tokw = sb("tokw", [P, KP, D])
        pos = sb("pos", [P, 2, D])
        rowsb = sb("rowsb", [P, 4, D])
        qkb = sb("qkb", [P, 2, QKC])
        col = sb("col", [P, 2, 2, 2])
        const = sb("const", [P, 2 * P + QUAD + 64])
        ident = const[:, 0:P]
        lower = const[:, P:P + 64].rearrange("p (e j) -> p e j", e=EXPERTS)
        mask_rows = sb("mask_rows", [P, P + QUAD], F32R)
        wide_hi = sb("wide_hi", [P, 4 * W_QKV], F32R)
        wide_lo = sb("wide_lo", [P, 4 * W_QKV], F32R)
        qkv_hi, qkv_lo = (w[:, :].rearrange("p (n m c) -> p n m c", n=2, m=2) for w in (wide_hi, wide_lo))
        w1_hi, w1_lo = (w[:, 0:4 * HID].rearrange("p (s c) -> p s c", s=2) for w in (wide_hi, wide_lo))
        out_hi = sb("out_hi", [P, 3, 2, PADN], F32R)
        out_lo = sb("out_lo", [P, 3, 2, PADN], F32R)
        b1c = sb("b1c", [P, EXPERTS, HC])
        b2r = sb("b2r", [EXPERTS, D])

        H = sb("H", [P, TILES, D])
        Y = sb("Y", [P, TILES, D])
        X = sb("X", [P, TILES, 2 * P])
        R = sb("R", [P, TILES, D])
        bn = sb("bn", [P, TILES, 6])
        mv = sb("mv", [P, TILES, 2])
        var_eps = sb("var_eps", [P, GROUPS, 2, GT])
        minus_half = sb("minus_half", [P, 2, GT])
        rstd = sb("rstd", [P, GROUPS, 2, GT])
        xt32 = sb("xt32", [P, 2, GN])
        xt_hi = sb("xt_hi", [P, GROUPS, GN], F32R)
        xt_lo = sb("xt_lo", [P, GROUPS, GN], F32R)
        xt_tail = sb("xt_tail", [P, GROUPS, GN], F32R)
        late = sb("late", [P, GROUPS * QKC * GN])
        qkT = late[:, :].rearrange("p (g c n) -> p g c n", g=GROUPS, c=QKC)
        raw_small = [late[:, 0:2 * W_QKV].rearrange("p (m c) -> p m c", m=2),
                     early[:, RAW:RAW + 2 * W_QKV].rearrange("p (m c) -> p m c", m=2)]
        raw_out = late[:, QKC * GN:QKC * GN + 6 * PADN].rearrange("p (w m c) -> p w m c", w=3, m=2)
        V = sb("V", [P, TILES, HEADS, VAUG])
        W_SC = HEADS * QUAD
        SC = PAIR * W_SC
        S = sb("S", [P, 2, SC])
        St = sb("St", [P, 2, SC])
        rowmax = sb("rowmax", [P, 2, PAIR * HEADS])
        rden = sb("rden", [P, 2, PAIR * HEADS])
        L = sb("L", [P, TILES, EXPERTS])
        Lx = sb("Lx", [P, TILES, EXPERTS])
        top = sb("top", [P, TILES])
        beats, ties = (S[:, b, 0:GT * EXPERTS * EXPERTS].rearrange("p (t e j) -> p t e j", t=GT, e=EXPERTS)
                       for b in range(2))
        rank = sb("rank", [P, TILES, EXPERTS])
        gates = sb("gates", [P, TILES, EXPERTS])
        gsum = sb("gsum", [P, TILES])
        gatesT = sb("gatesT", [EXPERTS, GROUPS, GN])
        w2s = sb("w2s", [P, 2, HC, 2 * D], F32R)
        NH = 4
        hid32 = late[:, 0:NH * GN].rearrange("p (k n) -> p k n", k=NH)
        hid_hi = sb("hid_hi", [P, NH, GN], F32R)
        hid_lo = sb("hid_lo", [P, NH, GN], F32R)

        psum = ctx.enter_context(nc.psum_tensor("psum", [P, 8, 512], F32))

        ld_tok, ld_pos, ld_const, ld_small, ld_out, ld_bias = (sem(n) for n in (
            "ld_tok", "ld_pos", "ld_const", "ld_small", "ld_out", "ld_bias"))
        ld_first = sem("ld_first")
        ld_x = [sem(f"ld_x{p}") for p in range(TILES // PAIR)]
        ld_e = [sem("ld_e0"), sem("ld_e1")]
        ring_full = sem("ring_full")
        ring_free = [sem("ring_free0"), sem("ring_free1")]
        turn_full, turn_free, turn_hi, main_out, xt_ready = (sem(n) for n in (
            "turn_full", "turn_free", "turn_hi", "main_out", "xt_ready"))
        o_ready, mask_ready, pool_chain = (sem(n) for n in ("o_ready", "mask_ready", "pool_chain"))
        post_done = [sem("post_done0"), sem("post_done1")]
        x_ready, var_ready, rstd_ready, setup = sem("x_ready"), sem("var_ready"), sem("rstd_ready"), sem("setup")
        small_hi, small_lo = sem("small_hi"), sem("small_lo")
        rows_done = sem("rows_done")
        score_full, shifted, exped, flipped = (sem(n) for n in (
            "score_full", "shifted", "exped", "flipped"))
        mix_full, mix_free, dve_chain = sem("mix_full"), sem("mix_free"), sem("dve_chain")
        logit_shifted, logit_exped, gates_ready = (sem(n) for n in (
            "logit_shifted", "logit_exped", "gates_ready"))
        exp_hi, exp_lo = sem("exp_hi"), sem("exp_lo")
        hid_act, hid_ready, hid_used = (sem(n) for n in ("hid_act", "hid_ready", "hid_used"))
        down_full, down_free, stored = sem("down_full"), sem("down_free"), sem("stored")

        def ring_bank(key):
            return psum[:, 2 + RING[key] % 2, :]

        def pair_view(bank, width):
            return bank.rearrange("p (t c) -> p t c", t=2)[:, :, 0:width]

        def ring_read(eng, key):
            eng.wait_ge(ring_free[RING[key] % 2], RING[key] // 2 + 1)

        block = ctx.enter_context(nc.Block())

        @block.sync
        def _(sp):
            def load_patches(p):
                sp.dma_start(patches[:, 2 * p:2 * p + 2], xT[:, 2 * p:2 * p + 2]).then_inc(ld_x[p], 16)

            sp.dma_start(patches[:, 0], xT[:, 0]).then_inc(ld_first, 16)
            sp.dma_start(patches[:, 1], xT[:, 1]).then_inc(ld_x[0], 16)
            load_patches(1)
            sp.dma_start(rowsb[:, :, :], rows).then_inc(ld_const, 16)
            sp.dma_start(qkb[:, :, :], qk_bias).then_inc(ld_const, 16)
            sp.dma_start(col[:, :, :, :], cols).then_inc(ld_const, 16)
            sp.dma_start(raw_small[0], wqkv[0]).then_inc(ld_small, 16)
            load_patches(2)
            load_patches(3)
            sp.dma_start(raw_out, wout).then_inc(ld_out, 16)
            sp.dma_start(b1c[:, :, :], b1).then_inc(ld_bias, 16)
            sp.dma_start(b2r[:, :], b2).then_inc(ld_bias, 16)
            sp.wait_ge(ring_full, RING["tok", 1, 1] + 1)
            sp.dma_start(raw_small[1], wqkv[1]).then_inc(ld_small, 16)
            for e in range(EXPERTS):
                if e == 1:
                    sp.wait_ge(small_lo, 3)
                if e >= 2:
                    sp.wait_ge(exp_lo, e - 1)
                sp.dma_start(raw_e[:, e % 2, :], w_exp[e]).then_inc(ld_e[e % 2], 16)
            for t in range(TILES):
                sp.wait_ge(down_free, (EXPERTS * GROUPS - GROUPS) * GT + t + 1)
                sp.dma_start(out[t], R[:, t, :]).then_inc(stored, 16)
            sp.wait_ge(stored, 16 * TILES)

        LD_CONST = 16 * 4

        def split_expert_lo(pool, e):
            s = e % 2
            pool.wait_ge(exp_hi, 2 * e + 2)
            nc.gpsimd.tensor_tensor(w1_lo[:, s, :], raw_e[:, s, 0:2 * HID], w1_hi[:, s, :].bitcast(F32), ALU.subtract)
            w2 = raw_e[:, s, 2 * HID:RAW].rearrange("p (c d) -> p c d", c=HC)
            nc.gpsimd.tensor_tensor(w2s[:, s, :, D:2 * D], w2, w2s[:, s, :, 0:D].bitcast(F32), ALU.subtract) \
                .then_inc(exp_lo, 1)

        @block.gpsimd
        def _(pool):
            nc.gpsimd.memset(minus_half[:, :, :], -0.5).then_inc(setup, 1)
            nc.gpsimd.memset(V[:, :, :, HD:VAUG], 1.0).then_inc(setup, 1)
            pool.wait_ge(setup, 2)
            norms = 0

            def root(g, twice):
                nonlocal norms
                norms += 1
                pool.wait_ge(var_ready, norms)
                m = 2 if twice else 1
                nc.gpsimd.tensor_tensor(rstd[:, g, 0:m], var_eps[:, g, 0:m], minus_half[:, 0:m], ALU.pow) \
                    .then_inc(rstd_ready, 1)

            def split_small(n):
                pool.wait_ge(small_hi, (1, 3)[n])
                nc.gpsimd.tensor_tensor(qkv_lo[:, n, :, :], raw_small[n], qkv_hi[:, n, :, :].bitcast(F32),
                                        ALU.subtract).then_inc(small_lo, 1)

            split_small(0)
            for stage in ORDER:
                if stage[0] == "ln":
                    root(stage[2], stage[1] == 2)
                elif stage[0] == "post":
                    if stage == ("post", 0, 0):
                        pool.wait_ge(ld_const, LD_CONST)
                    _, j, g = stage
                    pool.wait_ge(x_ready, 2 * LNS["ln", j, g] + 2)
                    s = slice(g * GT, g * GT + GT)
                    if j == 4:
                        ins = nc.gpsimd.tensor_tensor(R[:, s, :], H[:, s, :], Y[:, s, :], ALU.add)
                    else:
                        res, row = ((H, rowsb[:, 1, :]), (Y, rowsb[:, 3, :]))[j // 2]
                        if j == 2:
                            for i in range(GT):
                                t = g * GT + i
                                ins = nc.gpsimd.tensor_scalar(Y[:, t, :], H[:, t, :], mv[:, t, 0:1],
                                                              rstd[:, g, 0, i:i + 1], ALU.subtract, ALU.mult)
                            ins.then_inc(pool_chain, 1)
                            pool.wait_ge(pool_chain, g + 1)
                        ins = nc.gpsimd.tensor_tensor(res[:, s, :], res[:, s, :],
                                                      row.unsqueeze(1).to_broadcast([P, GT, D]), ALU.add)
                    ins.then_inc(post_done[g], 1)
                elif stage == ("turn", 0, 0):
                    pool.wait_ge(small_hi, 2)
                    nc.gpsimd.tensor_tensor(out_lo[:, :, :, :], raw_out, out_hi[:, :, :, :].bitcast(F32),
                                            ALU.subtract).then_inc(small_lo, 1)
                elif stage == ("low", 1):
                    split_small(1)
                elif stage[0] == "low":
                    split_expert_lo(pool, stage[1] - 2)

        def split_expert_hi(act, e):
            s = e % 2
            act.wait_ge(ld_e[s], 16 * (e // 2 + 1))
            if e >= 2:
                act.wait_ge(down_full, (e - 1) * GROUPS * GT)
            nc.scalar.activation(w1_hi[:, s, :], raw_e[:, s, 0:2 * HID], ACT.Copy).then_inc(exp_hi, 1)
            w2 = raw_e[:, s, 2 * HID:RAW].rearrange("p (c d) -> p c d", c=HC)
            nc.scalar.activation(w2s[:, s, :, 0:D], w2, ACT.Copy).then_inc(exp_hi, 1)

        def chunk_used(eng, j):
            if j % HC == HC - 1:
                eng.wait_ge(down_full, (j // HC + 1) * GT)
            else:
                eng.wait_ge(hid_used, j // HC * (HC - 1) + j % HC + 1)

        @block.scalar
        def _(act):
            act.dma_start(tokw[:, :, :], tok_w).then_inc(ld_tok, 16)
            act.dma_start(pos[:, :, :], posb).then_inc(ld_pos, 16)
            act.dma_start(const[:, :], consts).then_inc(ld_const, 16)
            act.wait_ge(ld_small, 16)
            nc.scalar.activation(qkv_hi[:, 0, :, :], raw_small[0], ACT.Copy).then_inc(small_hi, 1)
            act.wait_ge(ld_out, 16)
            nc.scalar.activation(out_hi[:, :, :, :], raw_out, ACT.Copy).then_inc(small_hi, 1)
            act.wait_ge(ld_const, LD_CONST)
            nc.scalar.activation(mask_rows[:, :], const[:, P + 64:], ACT.Copy).then_inc(mask_ready, 1)
            for stage in ORDER:
                kind = stage[0]
                if kind == "lift":
                    _, j, g = stage
                    u = TURNS["turn", j, g]
                    act.wait_ge(turn_full, u + 1)
                    for m, hi in ((1, xt_tail), (0, xt_hi)):
                        if j in (2, 4):
                            if m == 0:
                                act.wait_ge(main_out, AFFINE[j, g] + 1)
                            scale, bias = (col[:, j // 2 - 1, v, m:m + 1] for v in range(2))
                            ins = nc.scalar.activation(hi[:, g, :], psum[:, m, :], ACT.Identity, scale=scale, bias=bias)
                        else:
                            ins = nc.scalar.activation(hi[:, g, :], psum[:, m, :], ACT.Copy)
                        ins.then_inc(turn_hi, 1)
                elif kind == "qk":
                    _, n, g, c = stage
                    act.wait_ge(small_lo, g + 1)
                    act.wait_ge(ring_full, RING[stage] + 1)
                    nc.scalar.activation(qkT[:, g, c, :], ring_bank(stage), ACT.Identity,
                                         bias=qkb[:, n, c:c + 1]).then_inc(ring_free[RING[stage] % 2], 1)
                elif kind == "soft":
                    _, n, t = stage
                    tile = n * TILES + t
                    probs = S[:, tile // 2 % 2, t % 2 * W_SC:(t % 2 + 1) * W_SC]
                    act.wait_ge(shifted, tile + 1)
                    nc.scalar.activation(probs, probs, ACT.Exp, scale=SCALES[n]).then_inc(exped, 1)
                elif stage == ("high", 1):
                    act.wait_ge(ld_small, 32)
                    nc.scalar.activation(qkv_hi[:, 1, :, :], raw_small[1], ACT.Copy).then_inc(small_hi, 1)
                elif kind == "high":
                    if stage[1] == 2:
                        act.wait_ge(ring_full, RING["v", 1, 1, 1] + 1)
                    split_expert_hi(act, stage[1] - 2)
                elif kind == "gate":
                    g = stage[1]
                    s = slice(g * GT, g * GT + GT)
                    act.wait_ge(logit_shifted, g + 1)
                    nc.scalar.activation(Lx[:, s, :], Lx[:, s, :], ACT.Exp).then_inc(logit_exped, 1)
                elif kind == "gates":
                    g = stage[1]
                    act.wait_ge(turn_full, TURNS[stage] + 1)
                    nc.scalar.activation(gatesT[:, g, :], psum[0:EXPERTS, 0, :], ACT.Copy).then_inc(turn_free, 1)
                elif kind == "up":
                    k = stage[1]
                    e, c = k // (GROUPS * HC), k % HC
                    act.wait_ge(ring_full, RING[stage] + 1)
                    if k >= NH:
                        chunk_used(act, k - NH)
                    else:
                        act.wait_ge(ld_bias, 32)
                        act.wait_ge(score_full, TILES + GT)
                    bias = b1c[:, e, c:c + 1]
                    nc.scalar.activation(hid32[:, k % NH, :], ring_bank(stage), ACT.Gelu, bias=bias).then_inc(hid_act, 1)
                    nc.scalar.activation(hid_hi[:, k % NH, :], ring_bank(stage), ACT.Gelu, bias=bias) \
                        .then_inc(ring_free[RING[stage] % 2], 1)

        @block.vector
        def _(dve):
            chain = 0

            def link(ins):
                nonlocal chain
                chain += 1
                ins.then_inc(dve_chain, 1)
                dve.wait_ge(dve_chain, chain)

            norms = 0

            def moments(src, t):
                for i in (t, t + 1):
                    ins = nc.vector.bn_stats(bn[:, i, :], src[:, i, :])
                link(ins)
                for i in (t, t + 1):
                    ins = nc.vector.bn_aggr(mv[:, i, :], bn[:, i, :])
                return ins

            def normalise(src, g, twice):
                nonlocal norms
                s = slice(g * GT, g * GT + GT)
                ins = nc.vector.tensor_scalar(var_eps[:, g, 0, :], mv[:, s, 1], EPS, None, ALU.add)
                if twice:
                    ins = nc.vector.tensor_scalar(var_eps[:, g, 1, :], mv[:, s, 1], 1 + EPS, EPS ** 2, ALU.mult, ALU.add)
                ins.then_inc(var_ready, 1)
                norms += 1
                dve.wait_ge(rstd_ready, norms)
                for pair in (0, 2):
                    for i in (pair, pair + 1):
                        t = g * GT + i
                        factor = rstd[:, g, 1 if twice else 0, i:i + 1]
                        ins = nc.vector.tensor_scalar(X[:, t, 0:D], src[:, t, :], mv[:, t, 0:1], factor,
                                                      ALU.subtract, ALU.mult)
                    link(ins)
                    tail_twice(slice(t - 1, t + 1)).then_inc(x_ready, 1)

            def tail_twice(s):
                return nc.vector.tensor_copy(X[:, s, D:2 * P], X[:, s, P:D])

            dve.wait_ge(ld_pos, 16)
            link(nc.vector.tensor_tensor(pos[:, 0, :], pos[:, 0, :], pos[:, 1, :], ALU.add))
            dve.wait_ge(setup, 2)
            for stage in ORDER:
                kind = stage[0]
                if kind == "tok":
                    _, g, p = stage
                    t = g * GT + p * 2
                    dve.wait_ge(ring_full, RING[stage] + 1)
                    ins = nc.vector.tensor_tensor(H[:, t:t + 2, :], pair_view(ring_bank(stage), D),
                                                  pos[:, 0:1, :].to_broadcast([P, 2, D]), ALU.add)
                    ins.then_inc(ring_free[RING[stage] % 2], 1)
                    ring_read(dve, stage)
                    link(moments(H, t))
                elif kind == "ln":
                    _, j, g = stage
                    normalise((H, H, Y)[j // 2], g, j == 2)
                elif kind == "lift":
                    _, j, g = stage
                    dve.wait_ge(turn_full, TURNS["turn", j, g] + 1)
                    u = XT[j, g]
                    sides = ((1, TAIL, xt_tail[TAIL:P, g, :], xt_tail[TAIL:P, g, :]), (0, 0, xt_lo[:, g, :], xt_hi[:, g, :]))
                    if j in (2, 4):
                        for m, rows, _, _ in reversed(sides):
                            scale, bias = (col[rows:P, j // 2 - 1, v, m:m + 1] for v in range(2))
                            if m:
                                dve.wait_ge(turn_hi, 2 * u + 1)
                            ins = nc.vector.tensor_scalar(xt32[rows:P, m, :], psum[rows:P, m, :], scale, bias,
                                                          ALU.mult, ALU.add)
                            if m == 0:
                                ins.then_inc(main_out, 1)
                        link(ins)
                        dve.wait_ge(main_out, AFFINE[j, g] + 1)
                    for n, (m, rows, lo, hi) in enumerate(sides):
                        dve.wait_ge(turn_hi, 2 * u + n + 1)
                        full = xt32[rows:P, m, :] if j in (2, 4) else psum[rows:P, m, :]
                        ins = nc.vector.tensor_tensor(lo, full, hi.bitcast(F32), ALU.subtract)
                    ins.then_inc(xt_ready, 1)
                elif kind == "v":
                    _, n, g, p = stage
                    if (n, g, p) == (0, 0, 0):
                        dve.wait_ge(ld_const, LD_CONST)
                    dve.wait_ge(ring_full, RING[stage] + 1)
                    for i in range(2):
                        t = g * GT + 2 * p + i
                        src = pair_view(ring_bank(stage), D)[:, i, :].rearrange("p (h d) -> p h d", h=HEADS)
                        bias = rowsb[:, 2 * n, :].rearrange("p (h d) -> p h d", h=HEADS)
                        ins = nc.vector.tensor_tensor(V[:, t, :, 0:HD], src, bias, ALU.add)
                    ins.then_inc(ring_free[RING[stage] % 2], 1)
                elif kind == "soft":
                    _, n, t = stage
                    tile = n * TILES + t
                    b, i = tile // 2 % 2, t % 2
                    dve.wait_ge(score_full, tile + 1)
                    scores = psum[:, SCORE_BANKS[tile % 3], 0:W_SC].rearrange("p (x j) -> p x j", j=QUAD)
                    highest = rowmax[:, b, i * HEADS:(i + 1) * HEADS]
                    link(nc.vector.tensor_reduce(highest, scores, AX_X, ALU.max))
                    nc.vector.tensor_tensor(S[:, b, i * W_SC:(i + 1) * W_SC].rearrange("p (x j) -> p x j", j=QUAD), scores,
                                            highest.unsqueeze(2).to_broadcast([P, HEADS, QUAD]),
                                            ALU.subtract).then_inc(shifted, 1)
                elif kind == "flip":
                    _, n, p = stage
                    s = 4 * n + p
                    dve.wait_ge(exped, PAIR * (s + 1))
                    nc.vector.transpose(St[:, s % 2, :], S[:, s % 2, :]).then_inc(flipped, 1)
                elif kind == "norm":
                    _, n, p = stage
                    s = 4 * n + p
                    dve.wait_ge(mix_full, s + 1)
                    mixed = psum[:, MIX_BANK, 0:PAIR * HEADS * VAUG].rearrange("p (x d) -> p x d", d=VAUG)
                    link(nc.vector.reciprocal(rden[:, s % 2, :].unsqueeze(2), mixed[:, :, HD:VAUG]))
                    Xv = X[:, 2 * p:2 * p + 2, 0:D].rearrange("p t (h d) -> p t h d", h=HEADS)
                    mix = mixed[:, :, 0:HD].rearrange("p (t h) d -> p t h d", t=PAIR)
                    scale = rden[:, s % 2, :].rearrange("p (t h) -> p t h", t=PAIR).unsqueeze(3)
                    ins = nc.vector.tensor_tensor(Xv, mix, scale.to_broadcast([P, PAIR, HEADS, HD]), ALU.mult)
                    ins.then_inc(mix_free, 1)
                    dve.wait_ge(mix_free, s + 1)
                    tail_twice(slice(2 * p, 2 * p + 2)).then_inc(o_ready, 1)
                elif kind == "proj":
                    _, n, g, p = stage
                    res = (H, Y)[n]
                    t = g * GT + 2 * p
                    dve.wait_ge(post_done[g], n + 1)
                    dve.wait_ge(ring_full, RING[stage] + 1)
                    nc.vector.tensor_tensor(res[:, t:t + 2, :], pair_view(ring_bank(stage), D), res[:, t:t + 2, :],
                                            ALU.add).then_inc(ring_free[RING[stage] % 2], 1)
                    ring_read(dve, stage)
                    link(moments(res, t))
                elif kind == "gate":
                    g = stage[1]
                    s = slice(g * GT, g * GT + GT)
                    for p in range(2):
                        key = ("gate", g, p)
                        t = g * GT + 2 * p
                        dve.wait_ge(ring_full, RING[key] + 1)
                        nc.vector.tensor_copy(L[:, t:t + 2, :], pair_view(ring_bank(key), EXPERTS)) \
                            .then_inc(ring_free[RING[key] % 2], 1)
                        dve.wait_ge(ring_free[RING[key] % 2], RING[key] // 2 + 1)
                    link(nc.vector.tensor_reduce(top[:, s], L[:, s, :], AX_X, ALU.max))
                    nc.vector.tensor_tensor(Lx[:, s, :], L[:, s, :], top[:, s].unsqueeze(2).to_broadcast([P, GT, EXPERTS]),
                                            ALU.subtract).then_inc(logit_shifted, 1)
                    them = L[:, s, :].unsqueeze(2).to_broadcast([P, GT, EXPERTS, EXPERTS])
                    me = L[:, s, :].unsqueeze(3).to_broadcast([P, GT, EXPERTS, EXPERTS])
                    link(nc.vector.tensor_tensor(ties, them, me, ALU.is_equal))
                    link(nc.vector.tensor_tensor(ties, ties,
                                                 lower.unsqueeze(1).to_broadcast([P, GT, EXPERTS, EXPERTS]), ALU.mult))
                    link(nc.vector.tensor_tensor(beats, them, me, ALU.is_gt))
                    link(nc.vector.tensor_tensor(beats, beats, ties, ALU.add))
                    link(nc.vector.tensor_reduce(rank[:, s, :], beats, AX_X, ALU.add))
                    link(nc.vector.tensor_scalar(rank[:, s, :], rank[:, s, :], 1.5, None, ALU.is_lt))
                    dve.wait_ge(logit_exped, g + 1)
                    link(nc.vector.tensor_tensor(gates[:, s, :], rank[:, s, :], Lx[:, s, :], ALU.mult))
                    link(nc.vector.tensor_reduce(gsum[:, s], gates[:, s, :], AX_X, ALU.add))
                    link(nc.vector.reciprocal(gsum[:, s], gsum[:, s]))
                    nc.vector.tensor_tensor(gates[:, s, :], gates[:, s, :],
                                            gsum[:, s].unsqueeze(2).to_broadcast([P, GT, EXPERTS]),
                                            ALU.mult).then_inc(gates_ready, 1)
                elif kind == "gates":
                    g = stage[1]
                    dve.wait_ge(post_done[g], 3)
                    for p in range(2):
                        key = ("gates", g, p)
                        t = g * GT + 2 * p
                        dve.wait_ge(ring_full, RING[key] + 1)
                        nc.vector.tensor_tensor(R[:, t:t + 2, :], pair_view(ring_bank(key), D), R[:, t:t + 2, :],
                                                ALU.add).then_inc(ring_free[RING[key] % 2], 1)
                        ring_read(dve, key)
                elif kind == "up":
                    k = stage[1]
                    dve.wait_ge(hid_act, k + 1)
                    ring_read(dve, stage)
                    nc.vector.tensor_tensor(hid_lo[:, k % NH, :], hid32[:, k % NH, :],
                                            hid_hi[:, k % NH, :].bitcast(F32), ALU.subtract).then_inc(hid_ready, 1)
                elif kind == "add":
                    _, j, tiles = stage
                    e, g = j // GROUPS, j % GROUPS

                    def part(i, m):
                        t, u = g * GT + i, j * GT + i
                        acc = psum[:, ACC_BANKS[u % 6], m * D:m * D + D]
                        return nc.vector.scalar_tensor_tensor(R[:, t, :], acc, gates[:, t, e:e + 1], R[:, t, :],
                                                              ALU.mult, ALU.add)

                    if e:
                        dve.wait_ge(down_free, (j - GROUPS) * GT + tiles[-1] + 1)
                    first = chain
                    for i in tiles:
                        dve.wait_ge(down_full, j * GT + i + 1)
                        part(i, 0).then_inc(dve_chain, 1)
                        chain += 1
                    for n, i in enumerate(tiles):
                        dve.wait_ge(dve_chain, first + n + 1)
                        part(i, 1).then_inc(down_free, 1)

        @block.tensor
        def _(pe):
            def take_ring(key):
                m = RING[key]
                if m >= 2:
                    pe.wait_ge(ring_free[m % 2], m // 2)
                return ring_bank(key)

            def take_turn(stage):
                u = TURNS[stage]
                before = sum(TURNS[s] < u for s in TURNS if s[0] == "turn")
                if u > before:
                    pe.wait_ge(turn_free, u - before)
                if before:
                    pe.wait_ge(turn_hi, 2 * before)
                    pe.wait_ge(xt_ready, before)

            def project(key, g, p, w_hi, w_lo):
                bank = take_ring(key)
                for i in range(2):
                    o = bank[:, i * PADN:(i + 1) * PADN]
                    s = slice((2 * p + i) * P, (2 * p + i + 1) * P)
                    terms = [(xt_hi, w_hi[:, 0, :]), (xt_lo, w_hi[:, 0, :]), (xt_hi, w_lo[:, 0, :]),
                             (xt_tail, w_hi[:, 1, :]), (xt_tail, w_lo[:, 1, :])]
                    for j, (x, w) in enumerate(terms):
                        ins = nc.tensor.matmul(o, x[:, g, s], w, start=(j == 0), stop=(j == 4))
                ins.then_inc(ring_full, 1)

            pe.wait_ge(ld_tok, 16)
            for stage in ORDER:
                kind = stage[0]
                if kind == "tok":
                    _, g, p = stage
                    t = g * GT + 2 * p
                    bank = take_ring(stage)
                    for i in range(2):
                        pe.wait_ge(ld_first if t == 0 and i == 0 else ld_x[t // 2], 16)
                        for c in range(KP):
                            ins = nc.tensor.matmul(bank[:, i * PADN:i * PADN + D], patches[:, t + i, c, :],
                                                   tokw[:, c, :], start=(c == 0), stop=(c == KP - 1))
                    ins.then_inc(ring_full, 1)
                elif kind == "turn":
                    _, j, g = stage
                    take_turn(stage)
                    if j == 0 and g == 0:
                        pe.wait_ge(ld_const, LD_CONST)
                    for i in range(GT):
                        t = g * GT + i
                        if j % 2 == 0:
                            pe.wait_ge(x_ready, 2 * LNS["ln", j, g] + i // 2 + 1)
                        else:
                            pe.wait_ge(o_ready, 4 * (j // 2) + 2 * g + i // 2 + 1)
                        nc.tensor.transpose(psum[:, 0, i * P:(i + 1) * P], X[:, t, 0:P], ident)
                        ins = nc.tensor.transpose(psum[:, 1, i * P:(i + 1) * P], X[:, t, P:2 * P], ident)
                    ins.then_inc(turn_full, 1)
                elif kind == "qk":
                    _, n, g, c = stage
                    if c == 0:
                        pe.wait_ge(xt_ready, XT[2 * n, g] + 1)
                        pe.wait_ge(small_lo, (1, 3)[n])
                    bank = take_ring(stage)
                    s = slice(c * P, (c + 1) * P)
                    terms = [(qkv_hi[:, n, 0, s], xt_hi), (qkv_hi[:, n, 0, s], xt_lo), (qkv_lo[:, n, 0, s], xt_hi),
                             (qkv_hi[:, n, 1, s], xt_tail), (qkv_lo[:, n, 1, s], xt_tail)]
                    if n == 0:
                        terms = terms[3:] if c in (Q_CHUNK[2], K_CHUNK[2]) else terms[:3]
                    for j, (w, x) in enumerate(terms):
                        ins = nc.tensor.matmul(bank, w, x[:, g, :], start=(j == 0), stop=(j == len(terms) - 1))
                    ins.then_inc(ring_full, 1)
                elif kind == "v":
                    _, n, g, p = stage
                    s = slice(QKC * P, W_QKV)
                    project(stage, g, p, qkv_hi[:, n, :, s], qkv_lo[:, n, :, s])
                elif kind == "score":
                    _, n, t = stage
                    tile = n * TILES + t
                    g = t // GT
                    if t % GT == 0:
                        ring_read(pe, ("qk", n, g, QKC - 1))
                        ring_read(pe, ("qk", n, g, QKC - 2))
                    if tile == 0:
                        pe.wait_ge(mask_ready, 1)
                    if tile >= 3:
                        pe.wait_ge(shifted, tile - 2)
                    bank = psum[:, SCORE_BANKS[tile % 3], 0:W_SC].rearrange("p (r g j) -> p r g j", r=NQ, g=HG)
                    nc.tensor.matmul(bank.rearrange("p r g j -> p (r g) j"), mask_rows[:, 0:P],
                                     mask_rows[:, P:].unsqueeze(1).to_broadcast([P, HEADS, QUAD]),
                                     start=True, stop=True)
                    for turn in range(NQ):
                        for r in range(NQ):
                            if turn:
                                pe.wait_ge(rows_done, tile * NQ * (NQ - 1) + (turn - 1) * NQ + (r + 1) % NQ + 1)
                            rows = slice(r * QUAD, (r + 1) * QUAD)
                            a = (r + turn) % NQ
                            tok = t % GT * P + a * QUAD
                            for hg in range(HG):
                                ins = nc.tensor.matmul(
                                    bank[a * QUAD:(a + 1) * QUAD, r, hg, :],
                                    qkT[rows, g, Q_CHUNK[hg], tok:tok + QUAD], qkT[rows, g, K_CHUNK[hg], tok:tok + QUAD],
                                    start=False, stop=True, tile_position=(r * QUAD, a * QUAD), skip_group_check=True)
                            if turn < NQ - 1:
                                ins.then_inc(rows_done, 1)
                    ins.then_inc(score_full, 1)
                elif kind == "mix":
                    _, n, t = stage
                    s = (n * TILES + t) // PAIR
                    i = t % PAIR
                    if i == 0:
                        pe.wait_ge(flipped, s + 1)
                        ring_read(pe, ("v", n, t // GT, t % GT // PAIR))
                        if s:
                            pe.wait_ge(mix_free, s)
                    probs = St[:, s % 2, :].rearrange("p (t r g i) -> p t r g i", t=PAIR, r=NQ, g=HG)
                    for h in range(HEADS):
                        for a in range(NQ):
                            q = slice(a * QUAD, (a + 1) * QUAD)
                            o = psum[q, MIX_BANK, (i * HEADS + h) * VAUG:(i * HEADS + h + 1) * VAUG]
                            ins = nc.tensor.matmul(o, probs[q, i, h % NQ, h // NQ, :], V[q, t, h, :],
                                                   start=True, stop=True, tile_position=(a * QUAD, a * QUAD))
                    if i == 1:
                        ins.then_inc(mix_full, 1)
                elif kind == "proj":
                    _, n, g, p = stage
                    pe.wait_ge(xt_ready, XT[2 * n + 1, g] + 1)
                    pe.wait_ge(small_lo, 2)
                    project(stage, g, p, out_hi[:, n], out_lo[:, n])
                elif kind == "gate":
                    g = stage[1]
                    pe.wait_ge(xt_ready, XT[4, g] + 1)
                    for p in range(2):
                        project(("gate", g, p), g, p, out_hi[:, 2], out_lo[:, 2])
                elif kind == "gates":
                    g = stage[1]
                    pe.wait_ge(gates_ready, g + 1)
                    pe.wait_ge(ld_bias, 32)
                    take_turn(stage)
                    for i in range(GT):
                        ins = nc.tensor.transpose(psum[0:EXPERTS, 0, i * P:(i + 1) * P], gates[:, g * GT + i, :], ident)
                    ins.then_inc(turn_full, 1)
                    pe.wait_ge(turn_free, g + 1)
                    for p in range(2):
                        key = ("gates", g, p)
                        bank = take_ring(key)
                        for i in range(2):
                            s = slice((2 * p + i) * P, (2 * p + i + 1) * P)
                            ins = nc.tensor.matmul(bank[:, i * PADN:i * PADN + D], gatesT[:, g, s], b2r[:, :],
                                                   start=True, stop=True)
                        ins.then_inc(ring_full, 1)
                elif kind == "up":
                    k = stage[1]
                    e, g, c = k // (GROUPS * HC), k // HC % GROUPS, k % HC
                    w = e % 2
                    if k % (GROUPS * HC) == 0:
                        pe.wait_ge(exp_lo, e + 1)
                    if e == 0 and c == 0:
                        pe.wait_ge(xt_ready, XT[4, g] + 1)
                    bank = take_ring(stage)
                    m, tl = slice(c * P, (c + 1) * P), slice(HID + c * P, HID + (c + 1) * P)
                    terms = [(w1_hi[:, w, m], xt_hi), (w1_hi[:, w, m], xt_lo), (w1_lo[:, w, m], xt_hi),
                             (w1_hi[:, w, tl], xt_tail), (w1_lo[:, w, tl], xt_tail)]
                    for j, (wt, x) in enumerate(terms):
                        ins = nc.tensor.matmul(bank, wt, x[:, g, :], start=(j == 0), stop=(j == 4))
                    ins.then_inc(ring_full, 1)
                elif kind == "down":
                    k = stage[1]
                    e, g, c = k // (GROUPS * HC), k // HC % GROUPS, k % HC
                    w = e % 2
                    if k == STEPS - 2:
                        continue
                    pe.wait_ge(hid_ready, k + 1)
                    if k == 0:
                        pe.wait_ge(shifted, 2 * TILES)
                        pe.wait_ge(mix_free, TILES)
                    if k == HC:
                        pe.wait_ge(turn_free, GROUPS)
                        pe.wait_ge(xt_ready, len(XT))
                    for i in range(GT):
                        u = (e * GROUPS + g) * GT + i
                        if c == 0 and u >= 6:
                            pe.wait_ge(down_free, u - 5)
                        s = slice(i * P, (i + 1) * P)
                        acc = psum[:, ACC_BANKS[u % 6], :]
                        for k, c in ((k - 1, c - 1), (k, c)) if k == STEPS - 1 else ((k, c),):
                            nc.tensor.matmul(acc[:, 0:PADN], hid_lo[:, k % NH, s], w2s[:, w, c, 0:PADN],
                                             start=(c == 0), stop=(c == HC - 1))
                            ins = nc.tensor.matmul(acc[:, 0:2 * D], hid_hi[:, k % NH, s], w2s[:, w, c, :],
                                                   start=False, stop=(c == HC - 1), skip_group_check=True)
                        if c == HC - 1:
                            ins.then_inc(down_full, 1)
                    if c < HC - 1:
                        ins.then_inc(hid_used, 1)


def kernel(**inputs):
    import numpy as np
    import concourse.bacc as bacc
    from concourse import mybir as mb
    from concourse.bass_utils import run_bass_kernel_spmd

    a = {k: np.asarray(v) for k, v in inputs.items()}
    f = np.float32

    def main_tail(w, width):
        o = np.zeros((P, 2, width), f)
        o[:, 0, :w.shape[1]] = w[0:P]
        o[0:TAIL, 1, :w.shape[1]] = w[P:D]
        o[TAIL:P, 1, :w.shape[1]] = w[P:D]
        return o

    def spread(w, axis_rows):
        o = np.zeros((axis_rows, QKC, NQ, QUAD), f)
        w = w.reshape(axis_rows, 2, HG, NQ, HD)
        for part, chunks in enumerate((Q_CHUNK, K_CHUNK)):
            for hg in range(HG):
                o[:, chunks[hg], :, HALF[hg] * HD:(HALF[hg] + 1) * HD] = w[:, part, hg]
        return o.reshape(axis_rows, QKC * P)

    wq = a["L0_attn_W_qkv"].reshape(HEADS, HD, 3, HD)
    dense = np.zeros((HEADS, HD, 3, HEADS, HD), f)
    for h in range(HEADS):
        dense[h, :, :, h, :] = wq[h]
    qkv = [dense.reshape(D, 3 * D), a["L0_ffn_qkv_w"].T]
    bias = [a["L0_attn_b_qkv"].reshape(HEADS, 3, HD).transpose(1, 0, 2).reshape(1, 3 * D),
            a["L0_ffn_qkv_b"].reshape(1, 3 * D)]
    wqkv = np.stack([main_tail(np.concatenate([spread(w[:, 0:2 * D], D), w[:, 2 * D:]], 1), W_QKV) for w in qkv])
    qk_bias = np.stack([spread(b[:, 0:2 * D], 1).reshape(QKC, P).T for b in bias], 1)
    wout = np.stack([main_tail(w, PADN) for w in (a["L0_attn_W_out"], a["L0_ffn_proj_w"].T, a["L0_ffn_w_gate"])], 1)
    rows = np.stack([bias[0][0, 2 * D:], a["L0_attn_b_out"], bias[1][0, 2 * D:], a["L0_ffn_proj_b"]])
    rows = np.broadcast_to(rows, (P, 4, D))
    posb = np.stack([np.tile(a["L0_tok_pos_emb"], (P // SEQ, 1)), np.broadcast_to(a["L0_tok_b"], (P, D))], 1)
    cols = np.stack([np.stack([np.stack([v[0:P], np.concatenate([v[P:D], v[P:D]])], 1)
                               for v in (a[f"L0_ffn_{m}_w"], a[f"L0_ffn_{m}_b"])], 1) for m in ("norm1", "norm2")], 1)
    patches = a["x"].reshape(64, 4, 16, 4, 16, 3).transpose(0, 1, 3, 2, 4, 5).reshape(TILES, P, KP, P)
    w1 = a["L0_ffn_W1"]
    w_exp = np.concatenate([w1[:, 0:P], np.concatenate([w1[:, P:D], w1[:, P:D]], 1),
                            a["L0_ffn_W2"].reshape(EXPERTS, HC, P, D).transpose(0, 2, 1, 3).reshape(EXPERTS, P, HC * D)], 2)
    image = np.arange(P + QUAD) // SEQ % 2
    mask = np.zeros((P, P + QUAD))
    for row in range(2):
        mask[row] = np.where(image == row, 1.0, 0.0)
        mask[row, P:] = np.where(image[P:] == row, 0.0, -1e30)
    lower = np.broadcast_to(np.arange(EXPERTS)[None, :] < np.arange(EXPERTS)[:, None], (P, EXPERTS, EXPERTS))
    arrays = {
        "xT": patches.transpose(3, 0, 2, 1), "tok_w": a["L0_tok_W"].reshape(KP, P, D).transpose(1, 0, 2),
        "posb": posb, "wqkv": wqkv, "wout": wout, "qk_bias": qk_bias, "rows": rows, "cols": cols,
        "consts": np.concatenate([np.eye(P), lower.reshape(P, -1), mask], 1).astype(f),
        "w_exp": w_exp, "b1": a["L0_ffn_b1"].reshape(EXPERTS, HC, P).transpose(2, 0, 1), "b2": a["L0_ffn_b2"],
    }
    arrays = {f"in_{k}": np.ascontiguousarray(v) for k, v in arrays.items()}
    nc = bacc.Bacc("TRN2", target_bir_lowering=False, num_devices=1)
    args = [nc.dram_tensor(k, v.shape, mb.dt.from_np(v.dtype), kind="ExternalInput").ap() for k, v in arrays.items()]
    args.append(nc.dram_tensor("out_0", (TILES, P, D), mb.dt.float32, kind="ExternalOutput").ap())
    vit_moe_kernel(nc, *args)
    r = run_bass_kernel_spmd(nc, [arrays], core_ids=[0])
    return r.results[0]["out_0"].reshape(64, SEQ, D)
```
